# Optimizing a Trainium2 kernel written in Bass

```python
import numpy as np
import jax
import jax.numpy as jnp

def _softmax(x, axis=-1):
    return jax.nn.softmax(x, axis=axis)

def _gelu(x):
    return jax.nn.gelu(x, approximate=True)

def _silu(x):
    return jax.nn.silu(x)

def _sigmoid(x):
    return jax.nn.sigmoid(x)

def _layernorm(x, axis=-1, eps=1e-05):
    m = jnp.mean(x, axis=axis, keepdims=True)
    v = jnp.var(x, axis=axis, keepdims=True)
    return (x - m) / jnp.sqrt(v + eps)

def _scatter_add(tgt, idx, src, axis=0):
    return tgt.at[idx].add(src)

def _segment_sum(src, seg, n):
    return jax.ops.segment_sum(src, seg, n)
kernel_name = 'mk_gnn_resnorm_d1_gnn_r8_cd21a1'

def setup_inputs(seed: int=0):
    np.random.seed(seed)
    _w = jnp.asarray

    def _rec_inputs():
        import jax
        import jax.numpy as jnp
        _gk = jax.random.key(seed)
        x = -0.000202 + 1 * jax.random.normal(jax.random.fold_in(_gk, 1), (6250, 128), jnp.float32)
        _s = jax.random.randint(jax.random.fold_in(_gk, 2), (100000,), 0, 6250, jnp.int32)
        _d = jax.random.randint(jax.random.fold_in(_gk, 3), (100000,), 0, 6250, jnp.int32)
        _loop = jnp.arange(6250, dtype=jnp.int32)
        src = jnp.concatenate([_s, _d, _loop])
        dst = jnp.concatenate([_d, _s, _loop])
        _o = jnp.argsort(dst, stable=True)
        src = src[_o]
        dst = dst[_o]
        edge_attr_128 = 2.93046e-05 + 1.00006 * jax.random.normal(jax.random.fold_in(_gk, 11), (206250, 128), jnp.float32)
        return (x, src, dst, edge_attr_128)
    x, src, dst, edge_attr_128 = _rec_inputs()

    def _L0_gnn_setup():
        import jax, jax.numpy as jnp
        import numpy as np
        N_NODES = 6250
        N_EDGES = 80000
        D_NODE = 128
        D_EDGE = 128
        IN_NF = D_NODE + D_EDGE
        H_NF = 256
        OUT_NF = 128
        key = jax.random.key(seed)
        k1, k2, k3, k4, k5, k6, k7 = jax.random.split(key, 7)
        node_feats = jax.random.normal(k1, (N_NODES, D_NODE), dtype=jnp.float32)
        edge_index = jax.random.randint(k2, (2, N_EDGES), 0, N_NODES, dtype=jnp.int64)
        edge_attr = jax.random.normal(k3, (N_EDGES, D_EDGE), dtype=jnp.float32)
        s1 = 1.0 / np.sqrt(IN_NF)
        s2 = 1.0 / np.sqrt(H_NF)
        W1 = jax.random.uniform(k4, (IN_NF, H_NF), jnp.float32, -s1, s1)
        b1 = jax.random.uniform(k5, (H_NF,), jnp.float32, -s1, s1)
        W2 = jax.random.uniform(k6, (H_NF, OUT_NF), jnp.float32, -s2, s2)
        b2 = jax.random.uniform(k7, (OUT_NF,), jnp.float32, -s2, s2)
        return {'node_feats': node_feats, 'edge_index': edge_index, 'edge_attr': edge_attr, 'W1': W1, 'b1': b1, 'W2': W2, 'b2': b2}
    _L0_gnn_all = _L0_gnn_setup()
    _L0_gnn_in = {k: v for k, v in _L0_gnn_all.items() if k in ('W1', 'b1', 'W2', 'b2')}
    del _L0_gnn_all
    return {'x': x, 'src': src, 'dst': dst, 'edge_attr_128': edge_attr_128, 'L0_gnn_W1': _L0_gnn_in['W1'], 'L0_gnn_b1': _L0_gnn_in['b1'], 'L0_gnn_W2': _L0_gnn_in['W2'], 'L0_gnn_b2': _L0_gnn_in['b2']}

def reference(x, src, dst, edge_attr_128, L0_gnn_W1, L0_gnn_b1, L0_gnn_W2, L0_gnn_b2):
    import jax
    import jax.numpy as jnp

    def _L0_gnn_ref(node_feats, edge_index, edge_attr, W1, b1, W2, b2):
        import jax, jax.numpy as jnp
        import numpy as np
        N_NODES = 6250
        N_EDGES = 80000
        D_NODE = 128
        D_EDGE = 128
        IN_NF = D_NODE + D_EDGE
        H_NF = 256
        OUT_NF = 128
        row = edge_index[0]
        agg = jax.ops.segment_sum(edge_attr, row, num_segments=node_feats.shape[0])
        node_in = jnp.concatenate([node_feats, agg], axis=1)
        h = node_in @ W1 + b1
        out = h @ W2 + b2
        return out
    edge_index = jnp.stack([src, dst])
    x = _layernorm(x + _L0_gnn_ref(x, edge_index, edge_attr_128, L0_gnn_W1, L0_gnn_b1, L0_gnn_W2, L0_gnn_b2), axis=-1)
    return x

_drawn_inputs = setup_inputs


def setup_inputs(seed=0):
    import zlib

    import numpy as np

    out = dict(_drawn_inputs(seed))
    spreads = {}
    factors = {'L0_gnn_b1': 4.203}
    for name, (base, spread) in spreads.items():
        noise = np.random.default_rng([zlib.crc32(name.encode()), seed]).standard_normal(out[name].shape)
        drawn = base * np.exp(spread * noise) if base else spread * noise
        out[name] = jnp.asarray(drawn.astype(out[name].dtype))
    for name, factor in factors.items():
        out[name] = (out[name] * factor).astype(out[name].dtype)
    return out
```

```python
import concourse.bass as bass
from concourse import mybir
from contextlib import ExitStack


def bass_segment_sum_resnorm_kernel(nc, x, src, edge_attr, w1, b1, w2, b2, out):
    f32, i32, bf16 = mybir.dt.float32, mybir.dt.int32, mybir.dt.bfloat16
    ALU = mybir.AluOpType
    ACT = mybir.ActivationFunctionType

    P = 128
    NODES, D = x.shape
    EDGES = edge_attr.shape[0]
    HID = w1.shape[1]
    EPS = 1e-5
    DMA = 16

    GT = 3
    GROUPS = 8
    U = GT * GROUPS
    LOADS = 4
    LT = U // LOADS
    STEPS = EDGES // (P * U)
    COLS = STEPS * U
    REST = EDGES - P * COLS
    RT = -(-REST // P)
    LAST = REST - P * (RT - 1)
    REST_GROUPS = [(0, GT), (GT, RT)]
    E = len(REST_GROUPS)
    assert GT < RT <= 2 * GT and COLS + RT <= (STEPS + 1) * U

    TABLES = 4
    REST_TABLES = [0, 0, 0, 1]
    FIRST_TABLES = [0, 1, 0, 1] + [(2, 0, 1)[u % 3] for u in range(U - 5)] + [3]
    LOOP_TABLES = [u % TABLES for u in range(U)]
    END_TABLES = [u % (TABLES - 1) for u in range(U)]
    ROWS = NODES + P
    SPLIT = 64
    assert ROWS <= SPLIT * 256 and U % (2 * LOADS) == 0 and len(REST_TABLES) == RT

    DW = D + 1
    NT = NODES // P
    NREST = NODES - P * NT
    QT = 4
    SLOTS = 4
    assert NT % (QT * SLOTS) == 0 and NT + 2 < STEPS and STEPS % 8 == 3 and D == P and HID == 2 * P

    TURNS = NT // (QT * SLOTS)
    CHUNKS = NT // QT + 1
    part_loads = DMA * (TABLES - 1)

    def tiles_of(c):
        return 1 if c == 0 else QT

    def tile_of(c):
        return NT if c == 0 else (c - 1) * QT

    before = [(REST_TABLES + FIRST_TABLES).count(r) for r in range(TABLES)]
    in_step = [LOOP_TABLES.count(r) for r in range(TABLES)]
    before_end = [before[r] + (STEPS - 2) * in_step[r] for r in range(TABLES)]
    table_total = [before_end[r] + END_TABLES.count(r) for r in range(TABLES)]

    edges_v = edge_attr[0:P * COLS, :].rearrange("(p c) f -> p c f", p=P)
    src_v = src[0:P * COLS].rearrange("(p c) -> p c", p=P)
    x_v = x[0:P * NT, :].rearrange("(p n) f -> p n f", p=P)
    out_v = out[0:P * NT, :].rearrange("(p n) f -> p n f", p=P)
    tables = [nc.dram_tensor(f"table{r}", (ROWS, D), f32, kind="Internal").ap() for r in range(TABLES)]
    tables_v = [t[0:P * NT, :].rearrange("(p n) f -> p n f", p=P) for t in tables]
    ZW = ROWS // 6
    assert ROWS % 6 == 0 and (ROWS * D) // P == ROWS

    with ExitStack() as ctx:
        ctx.enter_context(nc.allow_non_contiguous_dma(reason="b1 as a column, src pieces"))

        def sb(name, shape, dt):
            return ctx.enter_context(nc.sbuf_tensor(name, shape, dt))

        def pb(name):
            return ctx.enter_context(nc.psum_tensor(name, [P, 512], f32))

        def sem(name):
            return ctx.enter_context(nc.semaphore(name))

        src_i = sb("src_i", [P, U + COLS], i32)
        src_hi = sb("src_hi", [P, U + COLS], i32)
        src_f = sb("src_f", [P, U + COLS], f32)
        hilo = sb("hilo", [P, STEPS + 1, 2, U], bf16)
        hilo_t = sb("hilo_t", [2 * U, STEPS + 1, P], bf16)
        pick_1 = sb("pick_1", [2 * U, U], bf16)
        pick = sb("pick", [2 * U, U, P], bf16)
        data = sb("data", [P, U, DW], f32)
        data_rest = sb("data_rest", [P, RT, DW], f32)
        same = sb("same", [P, 2, GT, P], f32)
        sums = sb("sums", [P, GROUPS + E, GT, DW], f32)
        flag = sb("flag", [P, 2, GT], f32)
        index = sb("index", [P, U + E * GT], i32)
        spare_i = sb("spare_i", [P, 1], i32)
        spare_f = sb("spare_f", [P, 1], f32)
        weight_i = sb("weight_i", [P, 1], i32)
        limit_i = sb("limit_i", [P, 1], i32)
        ident = sb("ident", [P, P], f32)
        ident_b = sb("ident_b", [P, P], bf16)
        zeros = sb("zeros", [P, ZW], f32)
        w1_sb = sb("w1_sb", [P, 2, HID], f32)
        w2_sb = sb("w2_sb", [P, 2, D], f32)
        b1_sb = sb("b1_sb", [P, 2], f32)
        b2_sb = sb("b2_sb", [1, D], f32)
        w1_t = sb("w1_t", [P, 4, P], f32)
        wab = sb("wab", [P, 2, D], f32)
        bias = sb("bias", [1, D], f32)
        ones = sb("ones", [1, P], f32)
        x_tile = sb("x_tile", [P, D], f32)
        x_rest = sb("x_rest", [P, D], f32)
        x_t = sb("x_t", [P, P], f32)
        y0 = sb("y0", [P, NT + 1, D], f32)
        early = sb("early", [P, NT + 1, D], f32)
        part = [sb(f"part{r}", [P, SLOTS, QT, D], f32) for r in range(TABLES - 1)]
        agg_t = sb("agg_t", [P, 2, QT * P], f32)
        z = sb("z", [P, 2, QT, D], f32)
        stats = sb("stats", [P, QT, 6], f32)
        mv = sb("mv", [P, 2, QT, 2], f32)
        std = sb("std", [P, 2, QT], f32)
        rstd = sb("rstd", [P, 2, QT], f32)
        shift = sb("shift", [P, 2, QT], f32)
        eps = sb("eps", [P, 1], f32)

        p_src = [pb("p_src0"), pb("p_src1")]
        p_sum = [pb("p_sum0"), pb("p_sum1")]
        p_prep = [pb("p_prep0"), pb("p_prep1")]
        p_xt = pb("p_xt")
        p_y = pb("p_y")
        weight = weight_i[:, :].bitcast(f32)
        limit = limit_i[:, :].bitcast(f32)

        src_loaded = sem("src_loaded")
        rest_loaded = sem("rest_loaded")
        weights_loaded = sem("weights_loaded")
        x_rest_loaded = sem("x_rest_loaded")
        x_loaded = sem("x_loaded")
        data_loaded = [sem(f"data_loaded{q}") for q in range(LOADS)]
        table_zeroed = [sem(f"table_zeroed{r}") for r in range(TABLES)]
        zeros_ready = sem("zeros_ready")
        fills_ready = sem("fills_ready")
        consts_ready = sem("consts_ready")
        ident_ready = sem("ident_ready")
        data_rest_loaded = sem("data_rest_loaded")
        pool_fills = sem("pool_fills")
        pool_step = sem("pool_step")
        pick_ready = sem("pick_ready")
        dve_step = sem("dve_step")
        hilo_ready = sem("hilo_ready")
        weights_ready = sem("weights_ready")
        prep_done = sem("prep_done")
        prep_copied = sem("prep_copied")
        src_spread = sem("src_spread")
        same_ready = sem("same_ready")
        summed = sem("summed")
        sums_ready = sem("sums_ready")
        flag_ready = sem("flag_ready")
        index_ready = sem("index_ready")
        landed = [sem(f"landed{r}") for r in range(TABLES)]
        w1_t_done = sem("w1_t_done")
        w1_t_ready = sem("w1_t_ready")
        wab_done = sem("wab_done")
        wab_ready = sem("wab_ready")
        x_t_done = sem("x_t_done")
        x_t_ready = sem("x_t_ready")
        y_done = sem("y_done")
        y0_ready = sem("y0_ready")
        part_loaded = [sem(f"part_loaded{s}") for s in range(SLOTS)]
        early_loaded = sem("early_loaded")
        half_added = sem("half_added")
        agg_ready = sem("agg_ready")
        agg_t_done = sem("agg_t_done")
        agg_t_ready = sem("agg_t_ready")
        map_done = sem("map_done")
        z_ready = sem("z_ready")
        stats_ready = sem("stats_ready")
        rstd_ready = sem("rstd_ready")
        quarter_added = sem("quarter_added")
        moments_ready = sem("moments_ready")
        std_ready = sem("std_ready")
        scale_ready = sem("scale_ready")
        result_ready = sem("result_ready")
        stored = sem("stored")

        block = ctx.enter_context(nc.Block())

        @block.sync
        def _(sp):
            sp.dma_start(src_i[:, U:U + COLS], src_v).then_inc(src_loaded, DMA)
            sp.wait_ge(pool_fills, 1)
            sp.dma_start(src_i[:, 0:RT - 1],
                         src[P * COLS:EDGES - LAST].rearrange("(p c) -> p c", p=P)).then_inc(rest_loaded, DMA)
            sp.dma_start(src_i[0:LAST, RT - 1:RT],
                         src[EDGES - LAST:EDGES].rearrange("(p c) -> p c", p=LAST)).then_inc(rest_loaded, DMA)
            sp.wait_ge(fills_ready, 1)
            sp.dma_start(data_rest[:, 0:RT - 1, 0:D],
                         edge_attr[P * COLS:EDGES - LAST, :].rearrange("(p c) f -> p c f", p=P)
                         ).then_inc(data_rest_loaded, DMA)
            sp.dma_start(data_rest[0:LAST, RT - 1, 0:D],
                         edge_attr[EDGES - LAST:EDGES, :]).then_inc(data_rest_loaded, DMA)
            for q in range(LOADS):
                sp.dma_start(data[:, q * LT:(q + 1) * LT, 0:D],
                             edges_v[:, q * LT:(q + 1) * LT, :]).then_inc(data_loaded[q], DMA)
            sp.dma_start(w1_sb[:, :, :], w1.rearrange("(k p) h -> p k h", p=P)).then_inc(weights_loaded, DMA)
            sp.dma_start(w2_sb[:, :, :], w2.rearrange("(k p) h -> p k h", p=P)).then_inc(weights_loaded, DMA)
            sp.dma_start(b1_sb[:, :], b1.rearrange("(k p) -> p k", p=P)).then_inc(weights_loaded, DMA)
            sp.dma_start(b2_sb[:, :], b2.rearrange("(o f) -> o f", o=1)).then_inc(weights_loaded, DMA)
            sp.dma_start(x_rest[0:NREST, :], x[P * NT:NODES, :]).then_inc(x_rest_loaded, DMA)
            sp.dma_start(x_tile[:, :], x_v[:, 0, :]).then_inc(x_loaded, DMA)

            def load_edges(step):
                for q in range(LOADS):
                    sp.wait_ge(summed, step * GROUPS + (E + (q + 1) * GROUPS // LOADS))
                    sp.dma_start(data[:, q * LT:(q + 1) * LT, 0:D],
                                 edges_v[:, bass.ds(step * U + (U + q * LT), LT), :]
                                 ).then_inc(data_loaded[q], DMA)

            load_edges(0)
            with sp.Fori(1, NT) as step:
                load_edges(step)
                sp.wait_ge(y0_ready, step + 1)
                sp.dma_start(x_tile[:, :], x_v[:, bass.ds(step, 1), :].rearrange("p n f -> p (n f)")
                             ).then_inc(x_loaded, DMA)
            with sp.Fori(NT, STEPS - 1) as step:
                load_edges(step)

            out_of_use = TABLES - 1
            sp.wait_ge(landed[out_of_use], DMA * table_total[out_of_use])
            sp.dma_start(early[:, NT, :], tables[out_of_use][P * NT:P * NT + P, :]).then_inc(early_loaded, DMA)
            for q in range(NT // QT):
                sp.wait_ge(landed[0], DMA * (before_end[0] + q // 2))
                sp.dma_start(early[:, q * QT:(q + 1) * QT, :], tables_v[out_of_use][:, q * QT:(q + 1) * QT, :]
                             ).then_inc(early_loaded, DMA)

            for r in range(TABLES - 1):
                sp.wait_ge(landed[r], DMA * table_total[r])
            for r in range(TABLES - 1):
                sp.dma_start(part[r][:, 0, 0, :], tables[r][P * NT:P * NT + P, :]).then_inc(part_loaded[0], DMA)

            def load_chunk(c, s):
                for r in range(TABLES - 1):
                    sp.dma_start(part[r][:, s, :, :], tables_v[r][:, bass.ds((c - 1) * QT, QT), :]
                                 ).then_inc(part_loaded[s], DMA)

            def store_chunk(c):
                sp.wait_ge(result_ready, c + 1)
                sp.dma_start(out_v[:, bass.ds((c - 1) * QT, QT), :], y0[:, bass.ds((c - 1) * QT, QT), :]
                             ).then_inc(stored, DMA)

            for c in range(1, SLOTS):
                load_chunk(c, c)
            sp.wait_ge(agg_t_done, 1)
            load_chunk(SLOTS, 0)
            sp.wait_ge(result_ready, 1)
            sp.dma_start(out[P * NT:NODES, :], y0[0:NREST, NT, :]).then_inc(stored, DMA)
            with sp.Fori(1, TURNS) as turn:
                for s in range(SLOTS):
                    c = turn * SLOTS + (s + 1)
                    sp.wait_ge(agg_t_done, c - (SLOTS - 1))
                    load_chunk(c, (s + 1) % SLOTS)
                    store_chunk(c - SLOTS)
            for c in range(CHUNKS - SLOTS, CHUNKS):
                store_chunk(c)
            sp.wait_ge(stored, DMA * CHUNKS)

        @block.gpsimd
        def _(pool):
            nc.gpsimd.iota(src_i[:, RT - 1:U], [[0, U - RT + 1]], base=NODES, channel_multiplier=1
                           ).then_inc(pool_fills, 1)
            nc.gpsimd.memset(ident_b[:, :], 0.0)
            nc.gpsimd.memset(pick_1[:, :], 0.0)
            nc.gpsimd.memset(ident[:, :], 0.0).then_inc(pool_step, 1)
            pool.wait_ge(pool_step, 1)
            nc.gpsimd.affine_select(out=pick_1[:, :], in_=pick_1[:, :], compare_op=ALU.not_equal, fill=1.0,
                                    base=0, pattern=[[-1, U]], channel_multiplier=1).then_inc(pool_step, 1)
            pool.wait_ge(pool_step, 2)
            nc.gpsimd.affine_select(out=pick_1[:, :], in_=pick_1[:, :], compare_op=ALU.not_equal, fill=1.0,
                                    base=-U, pattern=[[-1, U]], channel_multiplier=1).then_inc(pool_step, 1)
            nc.gpsimd.affine_select(out=ident_b[:, :], in_=ident_b[:, :], compare_op=ALU.not_equal, fill=1.0,
                                    base=0, pattern=[[-1, P]], channel_multiplier=1)
            nc.gpsimd.iota(spare_i[:, :], [[0, 1]], base=NODES, channel_multiplier=1)
            nc.gpsimd.iota(weight_i[:, :], [[0, 1]], base=(127 + 60) << 23, channel_multiplier=-(1 << 23))
            nc.gpsimd.iota(limit_i[:, :], [[0, 1]], base=((127 + 61) << 23) + (1 << 21),
                           channel_multiplier=-(1 << 23)).then_inc(consts_ready, 1)
            nc.gpsimd.affine_select(out=ident[:, :], in_=ident[:, :], compare_op=ALU.not_equal, fill=1.0,
                                    base=0, pattern=[[-1, P]], channel_multiplier=1).then_inc(ident_ready, 1)

            def scatter(slot, r, done, group_count):
                pool.wait_ge(table_zeroed[r], DMA)
                if group_count is not None:
                    pool.wait_ge(index_ready, group_count)
                if not (isinstance(done, int) and done == 0):
                    pool.wait_ge(landed[r], done)
                pool.indirect_dma_start(
                    out=tables[r][:, :], out_offset=bass.IndirectOffsetOnAxis(ap=index[:, slot:slot + 1], axis=0),
                    in_=sums[:, slot // GT, slot % GT, 0:D], in_offset=None,
                    compute_op=ALU.add).then_inc(landed[r], DMA)

            for t, r in enumerate(REST_TABLES):
                scatter(U + t, r, DMA * REST_TABLES[:t].count(r), t // GT + 1 if t % GT == 0 else None)
            for u, r in enumerate(FIRST_TABLES):
                scatter(u, r, DMA * (REST_TABLES + FIRST_TABLES[:u]).count(r),
                        E + u // GT + 1 if u % GT == 0 else None)

            landed_count = [pool.alloc_register(f"landed_count{r}") for r in range(TABLES)]
            index_count = pool.alloc_register("index_count")
            for r in range(TABLES):
                pool.reg_mov(landed_count[r], DMA * (before[r] - 1))
            pool.reg_mov(index_count, E + GROUPS)
            assert all(n > 0 for n in before)
            with pool.Fori(1, STEPS - 1) as step:
                for u, r in enumerate(LOOP_TABLES):
                    pool.reg_add(landed_count[r], landed_count[r], DMA)
                    if u % GT == 0:
                        pool.reg_add(index_count, index_count, 1)
                    scatter(u, r, landed_count[r], index_count if u % GT == 0 else None)
            for u, r in enumerate(END_TABLES):
                scatter(u, r, DMA * (before_end[r] + END_TABLES[:u].count(r)),
                        E + (STEPS - 1) * GROUPS + u // GT + 1 if u % GT == 0 else None)

            def add_half(s, n, loads):
                pool.wait_ge(part_loaded[s], loads)
                nc.gpsimd.tensor_tensor(out=part[1][:, s, 0:n, :], in0=part[1][:, s, 0:n, :],
                                        in1=part[2][:, s, 0:n, :], op=ALU.add).then_inc(half_added, 1)

            for c in range(SLOTS):
                add_half(c, tiles_of(c), part_loads)
            with pool.Fori(1, TURNS) as turn:
                for s in range(SLOTS):
                    add_half(s, QT, turn * part_loads + part_loads)
            add_half(0, QT, part_loads * (TURNS + 1))

        @block.scalar
        def _(act):
            act.wait_ge(zeros_ready, 1)
            act.wait_ge(src_loaded, DMA)
            for r in range(TABLES):
                act.dma_start(tables[r].rearrange("a f -> (a f)").rearrange("(p b c) -> p b c", p=P, b=6),
                              zeros[:, :].unsqueeze(1).to_broadcast([P, 6, ZW])).then_inc(table_zeroed[r], DMA)
            act.wait_ge(pool_step, 3)
            nc.scalar.copy(pick[:, :, :], pick_1[:, :].unsqueeze(2).to_broadcast([2 * U, U, P])).then_inc(pick_ready, 1)

            def copy_prep(first, i, count):
                act.wait_ge(prep_done, count)
                nc.scalar.copy(hilo_t[:, bass.ds(first, 4), :],
                               p_prep[i][0:2 * U, :].rearrange("p (b c) -> p b c", c=P)).then_inc(prep_copied, 1)

            copy_prep(0, 0, 1)

            def take_sums(slot, bank, tiles, count):
                act.wait_ge(summed, count)
                nc.scalar.copy(sums[:, slot, 0:tiles, :], p_sum[bank][:, 0:tiles * DW].rearrange(
                    "p (t c) -> p t c", c=DW)).then_inc(sums_ready, 1)

            for e, (t0, t1) in enumerate(REST_GROUPS):
                take_sums(GROUPS + e, e, t1 - t0, e + 1)
            for k in range(GROUPS):
                take_sums(k, k % 2, GT, E + k + 1)

            with act.Fori(0, STEPS // 8) as turn:
                for i in range(2):
                    copy_prep(turn * 8 + (4 + 4 * i), 1 - i, turn * 2 + (i + 2))

            act.wait_ge(w1_t_done, 1)
            nc.scalar.copy(w1_t[:, :, :], p_xt[:, :].rearrange("p (b c) -> p b c", c=P)).then_inc(w1_t_ready, 1)
            act.wait_ge(wab_done, 1)
            nc.scalar.copy(wab[:, :, :], p_y[:, 0:2 * D].rearrange("p (b c) -> p b c", c=D))
            nc.scalar.copy(bias[:, :], p_y[0:1, 2 * D:3 * D]).then_inc(wab_ready, 1)

            def copy_x_t(n):
                act.wait_ge(x_t_done, n + 1)
                act.wait_ge(y_done, n)
                nc.scalar.copy(x_t[:, :], p_xt[:, 0:P]).then_inc(x_t_ready, 1)

            copy_x_t(0)

            def steps(step, slot_landed, node):
                for k in range(GROUPS):
                    for u in range(k * GT, (k + 1) * GT):
                        act.wait_ge(*slot_landed(u))
                    take_sums(k, k % 2, GT, step * GROUPS + (E + k + 1))
                    if node and k == 1:
                        copy_x_t(step)

            def after_first(u):
                r = FIRST_TABLES[u]
                return landed[r], DMA * (REST_TABLES + FIRST_TABLES[:u + 1]).count(r)

            def after(step):
                def slot_landed(u):
                    r = LOOP_TABLES[u]
                    return landed[r], (step - 2) * (DMA * in_step[r]) + DMA * (
                        before[r] + LOOP_TABLES[:u + 1].count(r))
                return slot_landed

            steps(1, after_first, True)
            with act.Fori(2, NT + 1) as step:
                steps(step, after(step), True)
            with act.Fori(NT + 1, STEPS - 1) as step:
                steps(step, after(step), False)
            steps(STEPS - 1, after(STEPS - 1), False)

            def copy_agg_t(s, n, count):
                act.wait_ge(agg_t_done, count + 1)
                if not (isinstance(count, int) and count < 2):
                    act.wait_ge(map_done, count - 1)
                nc.scalar.copy(agg_t[:, s % 2, 0:n * P], p_prep[s % 2][:, 0:n * P]).then_inc(agg_t_ready, 1)

            def root(s, n, count):
                act.wait_ge(moments_ready, count + 1)
                nc.scalar.activation(std[:, s % 2, 0:n], mv[:, s % 2, 0:n, 1], ACT.Sqrt, bias=eps[:, :]
                                     ).then_inc(std_ready, 1)

            def normalise(c, s, n, tile):
                act.wait_ge(scale_ready, c + 1)
                for t in range(n):
                    last = nc.scalar.activation(y0[:, bass.ds(tile + t, 1), :].rearrange("p n f -> p (n f)"),
                                                z[:, s % 2, t, :], ACT.Identity,
                                                bias=shift[:, s % 2, t:t + 1], scale=rstd[:, s % 2, t:t + 1])
                last.then_inc(result_ready, 1)

            for c in range(SLOTS):
                copy_agg_t(c, tiles_of(c), c)
                if c >= 1:
                    root(c - 1, tiles_of(c - 1), c - 1)
                if c >= 2:
                    normalise(c - 2, c - 2, tiles_of(c - 2), tile_of(c - 2))
            with act.Fori(1, TURNS) as turn:
                for s in range(SLOTS):
                    c = turn * SLOTS + s
                    copy_agg_t(s, QT, c)
                    root((s - 1) % SLOTS, QT, c - 1)
                    normalise(c - 2, (s - 2) % SLOTS, QT, (c - 3) * QT)
            copy_agg_t(0, QT, CHUNKS - 1)
            root(SLOTS - 1, QT, CHUNKS - 2)
            normalise(CHUNKS - 3, SLOTS - 2, QT, tile_of(CHUNKS - 3))
            root(0, QT, CHUNKS - 1)
            normalise(CHUNKS - 2, SLOTS - 1, QT, tile_of(CHUNKS - 2))
            normalise(CHUNKS - 1, 0, QT, tile_of(CHUNKS - 1))

        @block.vector
        def _(dve):
            nc.vector.memset(zeros[:, :], 0.0).then_inc(zeros_ready, 1)
            nc.vector.memset(data_rest[:, RT - 1, :], 0.0)
            nc.vector.memset(x_rest[:, :], 0.0).then_inc(fills_ready, 1)
            nc.vector.memset(ones[:, :], 1.0)
            nc.vector.memset(eps[:, :], EPS)
            dve.wait_ge(src_loaded, DMA)
            dve.wait_ge(rest_loaded, 2 * DMA)
            for i, (b0, b1_) in enumerate(((0, 4), (4, STEPS + 1))):
                c0, c1 = b0 * U, b1_ * U
                hi = src_hi[:, c0:c1]
                nc.vector.tensor_scalar(hi, src_i[:, c0:c1], -SPLIT, None, ALU.bitwise_and).then_inc(dve_step, 1)
                nc.vector.tensor_copy(src_f[:, c0:c1], src_i[:, c0:c1])
                dve.wait_ge(dve_step, i + 1)
                hi = hi.rearrange("p (b w) -> p b w", w=U)
                nc.vector.tensor_copy(hilo[:, b0:b1_, 0, :], hi)
                nc.vector.tensor_tensor(hilo[:, b0:b1_, 1, :], src_i[:, c0:c1].rearrange("p (b w) -> p b w", w=U),
                                        hi, ALU.subtract).then_inc(hilo_ready, 1)
                if i == 0:
                    dve.wait_ge(consts_ready, 1)
                    nc.vector.tensor_copy(spare_f[:, :], spare_i[:, :])
                    nc.vector.tensor_copy(data_rest[:, :, D:DW], weight.unsqueeze(1).to_broadcast([P, RT, 1]))
                    nc.vector.tensor_copy(data[:, :, D:DW], weight.unsqueeze(1).to_broadcast([P, U, 1])
                                          ).then_inc(weights_ready, 1)
            dve.wait_ge(weights_ready, 1)
            dve.wait_ge(hilo_ready, 2)

            def compare(k, tiles, col, group):
                dve.wait_ge(src_spread, group + 1)
                if not (isinstance(group, int) and group < 2):
                    dve.wait_ge(summed, group - 1)
                nc.vector.tensor_tensor(
                    same[:, k % 2, 0:tiles, :], p_src[k % 2][:, 0:tiles * P].rearrange("p (t c) -> p t c", c=P),
                    src_f[:, bass.ds(col, tiles)].unsqueeze(2).to_broadcast([P, tiles, P]), ALU.is_equal
                ).then_inc(same_ready, 1)

            def rows(k, tiles, col, group):
                dve.wait_ge(sums_ready, group + 1)
                nc.vector.tensor_scalar(flag[:, k % 2, 0:tiles], sums[:, k, 0:tiles, D], limit, spare_f[:, :],
                                        ALU.is_gt, ALU.mult).then_inc(flag_ready, 1)
                dve.wait_ge(flag_ready, group + 1)
                nc.vector.tensor_tensor(index[:, k * GT:k * GT + tiles], flag[:, k % 2, 0:tiles],
                                        src_f[:, bass.ds(col, tiles)], ALU.max).then_inc(index_ready, 1)

            def add_y0(n, tile, x_used):
                dve.wait_ge(y_done, n + 1)
                nc.vector.tensor_tensor(y0[:, bass.ds(tile, 1), :].rearrange("p n f -> p (n f)"),
                                        p_y[:, 0:D], x_used[:, :], ALU.add).then_inc(y0_ready, 1)

            for e, (t0, t1) in enumerate(REST_GROUPS):
                compare(GROUPS + e, t1 - t0, t0, e)
                if e:
                    rows(GROUPS + e - 1, GT, 0, e - 1)
            rows(GROUPS + E - 1, RT - GT, GT, E - 1)

            def steps(step, node):
                for k in range(GROUPS):
                    compare(k, GT, step * U + (U + k * GT), step * GROUPS + (E + k))
                    if k:
                        rows(k - 1, GT, step * U + (U + (k - 1) * GT), step * GROUPS + (E + k - 1))
                    if node and k == 5:
                        add_y0(step, step - 1, x_tile)
                rows(GROUPS - 1, GT, step * U + (U + (GROUPS - 1) * GT), step * GROUPS + (E + GROUPS - 1))

            steps(0, False)
            add_y0(0, NT, x_rest)
            with dve.Fori(1, NT + 1) as step:
                steps(step, True)
            with dve.Fori(NT + 1, STEPS) as step:
                steps(step, False)

            dve.wait_ge(early_loaded, DMA * (NT // QT + 1))

            def add_parts(c, s, n, loads, tile):
                dve.wait_ge(part_loaded[s], loads)
                nc.vector.tensor_tensor(part[0][:, s, 0:n, :], part[0][:, s, 0:n, :], early[:, bass.ds(tile, n), :],
                                        ALU.add).then_inc(quarter_added, 1)
                dve.wait_ge(quarter_added, c + 1)
                dve.wait_ge(half_added, c + 1)
                nc.vector.tensor_tensor(part[0][:, s, 0:n, :], part[0][:, s, 0:n, :], part[1][:, s, 0:n, :],
                                        ALU.add).then_inc(agg_ready, 1)

            def moments(c, s, n, tile):
                dve.wait_ge(map_done, c + 1)
                if not (isinstance(c, int) and c < 2):
                    dve.wait_ge(result_ready, c - 1)
                nc.vector.tensor_tensor(z[:, s % 2, 0:n, :], p_src[s % 2][:, 0:n * D].rearrange(
                    "p (t c) -> p t c", c=D), y0[:, bass.ds(tile, n), :], ALU.add).then_inc(z_ready, 1)
                dve.wait_ge(z_ready, c + 1)
                for t in range(n):
                    last = nc.vector.bn_stats(stats[:, t, :], z[:, s % 2, t, :])
                last.then_inc(stats_ready, 1)

            def aggregate(c, s, n):
                for t in range(n):
                    last = nc.vector.bn_aggr(mv[:, s % 2, t, :], stats[:, t, :])
                last.then_inc(moments_ready, 1)

            def scales(c, s, n):
                dve.wait_ge(std_ready, c + 1)
                dve.wait_ge(stats_ready, min(c + 2, CHUNKS) if isinstance(c, int) else c + 2)
                nc.vector.reciprocal(rstd[:, s % 2, 0:n], std[:, s % 2, 0:n]).then_inc(rstd_ready, 1)
                if not (isinstance(c, int) and c + 1 == CHUNKS):
                    aggregate(c + 1, (s + 1) % SLOTS, tiles_of(c + 1) if isinstance(c, int) else QT)
                dve.wait_ge(rstd_ready, c + 1)
                nc.vector.scalar_tensor_tensor(shift[:, s % 2, 0:n], mv[:, s % 2, 0:n, 0], -1.0, rstd[:, s % 2, 0:n],
                                               ALU.mult, ALU.mult).then_inc(scale_ready, 1)

            for c in range(SLOTS):
                add_parts(c, c, tiles_of(c), part_loads, tile_of(c))
                if c >= 1:
                    moments(c - 1, c - 1, tiles_of(c - 1), tile_of(c - 1))
                if c == 1:
                    dve.wait_ge(stats_ready, 1)
                    aggregate(0, 0, tiles_of(0))
                if c >= 2:
                    scales(c - 2, c - 2, tiles_of(c - 2))
            with dve.Fori(1, TURNS) as turn:
                for s in range(SLOTS):
                    c = turn * SLOTS + s
                    add_parts(c, s, QT, turn * part_loads + part_loads, (c - 1) * QT)
                    moments(c - 1, (s - 1) % SLOTS, QT, (c - 2) * QT)
                    scales(c - 2, (s - 2) % SLOTS, QT)
            add_parts(CHUNKS - 1, 0, QT, part_loads * (TURNS + 1), tile_of(CHUNKS - 1))
            moments(CHUNKS - 2, SLOTS - 1, QT, tile_of(CHUNKS - 2))
            scales(CHUNKS - 3, SLOTS - 2, QT)
            moments(CHUNKS - 1, 0, QT, tile_of(CHUNKS - 1))
            scales(CHUNKS - 2, SLOTS - 1, QT)
            scales(CHUNKS - 1, 0, QT)

        @block.tensor
        def _(pe):
            pe.wait_ge(consts_ready, 1)
            pe.wait_ge(hilo_ready, 1)

            def prepare(first, i):
                for b in range(4):
                    last = nc.tensor.matmul(
                        p_prep[i][0:2 * U, b * P:(b + 1) * P],
                        lhsT=hilo[:, bass.ds(first + b, 1), :, :].rearrange("p b h u -> p (b h u)"),
                        rhs=ident_b[:, :], start=True, stop=True)
                last.then_inc(prep_done, 1)

            prepare(0, 0)
            def turn_x(n, x_used):
                nc.tensor.transpose(p_xt[:, 0:P], x_used[:, :], ident[:, :]).then_inc(x_t_done, 1)

            def map_x(n):
                pe.wait_ge(x_t_ready, n + 1)
                pe.wait_ge(y0_ready, n)
                nc.tensor.matmul(p_y[:, 0:D], lhsT=x_t[:, :], rhs=wab[:, 0, :], start=True, stop=False)
                nc.tensor.matmul(p_y[:, 0:D], lhsT=ones[:, :], rhs=bias[:, :], start=False, stop=True
                                 ).then_inc(y_done, 1)

            pe.wait_ge(prep_copied, 1)
            pe.wait_ge(pick_ready, 1)

            def spread(k, tiles, block_at):
                for t in range(tiles):
                    last = nc.tensor.matmul(
                        p_src[k % 2][:, t * P:(t + 1) * P],
                        lhsT=pick[:, k * GT + t, :],
                        rhs=hilo_t[:, bass.ds(block_at, 1), :].rearrange("q b j -> q (b j)"), start=True, stop=True)
                last.then_inc(src_spread, 1)

            def add_up(k, tiles, rows_of, group):
                pe.wait_ge(same_ready, group + 1)
                if not (isinstance(group, int) and group < 2):
                    pe.wait_ge(sums_ready, group - 1)
                for t in range(tiles):
                    last = nc.tensor.matmul(p_sum[k % 2][:, t * DW:(t + 1) * DW], lhsT=same[:, k % 2, t, :],
                                            rhs=rows_of[:, t, :], start=True, stop=True)
                last.then_inc(summed, 1)

            for e, (t0, t1) in enumerate(REST_GROUPS):
                for t in range(t0, t1):
                    last = nc.tensor.matmul(p_src[e][:, (t - t0) * P:(t - t0 + 1) * P], lhsT=pick[:, t, :],
                                            rhs=hilo_t[:, 0, :], start=True, stop=True)
                last.then_inc(src_spread, 1)
            pe.wait_ge(weights_ready, 1)
            pe.wait_ge(data_rest_loaded, 2 * DMA)
            for e, (t0, t1) in enumerate(REST_GROUPS):
                add_up(e, t1 - t0, data_rest[:, t0:t1, :], e)

            def steps(step, node):
                for k in range(GROUPS):
                    group = step * GROUPS + (E + k)
                    if k == 0:
                        spread(0, GT, step + 1)
                    if k + 1 < GROUPS:
                        spread(k + 1, GT, step + 1)
                    if k % (GROUPS // LOADS) == 0:
                        pe.wait_ge(data_loaded[k // (GROUPS // LOADS)], step * DMA + DMA)
                    add_up(k, GT, data[:, k * GT:(k + 1) * GT, :], group)
                    if node and k == 0:
                        pe.wait_ge(x_loaded, step * DMA)
                        turn_x(step, x_tile)
                    if node and k == 3:
                        map_x(step)

            steps(0, False)

            pe.wait_ge(hilo_ready, 2)
            with pe.Fori(0, STEPS // 8) as turn:
                for i in range(2):
                    pe.wait_ge(prep_copied, turn * 2 + 1)
                    prepare(turn * 8 + (4 + 4 * i), 1 - i)

            pe.wait_ge(weights_loaded, 4 * DMA)
            pe.wait_ge(ident_ready, 1)
            for k in range(2):
                for h in range(2):
                    last = nc.tensor.transpose(p_xt[:, (2 * k + h) * P:(2 * k + h + 1) * P],
                                               w1_sb[:, k, h * P:(h + 1) * P], ident[:, :])
            last.then_inc(w1_t_done, 1)
            pe.wait_ge(w1_t_ready, 1)
            for k in range(2):
                for h in range(2):
                    nc.tensor.matmul(p_y[:, k * D:(k + 1) * D], lhsT=w1_t[:, 2 * k + h, :], rhs=w2_sb[:, h, :],
                                     start=(h == 0), stop=(h == 1))
            for h in range(2):
                nc.tensor.matmul(p_y[0:1, 2 * D:3 * D], lhsT=b1_sb[:, h:h + 1], rhs=w2_sb[:, h, :],
                                 start=(h == 0), stop=False)
            nc.tensor.matmul(p_y[0:1, 2 * D:3 * D], lhsT=ones[0:1, 0:1], rhs=b2_sb[:, :],
                             start=False, stop=True).then_inc(wab_done, 1)

            pe.wait_ge(wab_ready, 1)
            pe.wait_ge(x_rest_loaded, DMA)
            turn_x(0, x_rest)
            map_x(0)
            pe.wait_ge(prep_copied, STEPS // 4 + 1)

            with pe.Fori(1, NT + 1) as step:
                steps(step, True)
            with pe.Fori(NT + 1, STEPS) as step:
                steps(step, False)

            pe.wait_ge(same_ready, STEPS * GROUPS + E)
            def map_chunk(c, s, n):
                pe.wait_ge(agg_ready, c + 1)
                if not (isinstance(c, int) and c < 2):
                    pe.wait_ge(agg_t_ready, c - 1)
                for t in range(n):
                    last = nc.tensor.transpose(p_prep[s % 2][:, t * P:(t + 1) * P], part[0][:, s, t, :], ident[:, :])
                last.then_inc(agg_t_done, 1)
                pe.wait_ge(agg_t_ready, c + 1)
                if not (isinstance(c, int) and c < 2):
                    pe.wait_ge(z_ready, c - 1)
                for t in range(n):
                    last = nc.tensor.matmul(p_src[s % 2][:, t * D:(t + 1) * D],
                                            lhsT=agg_t[:, s % 2, t * P:(t + 1) * P], rhs=wab[:, 1, :],
                                            start=True, stop=True)
                last.then_inc(map_done, 1)

            for c in range(SLOTS):
                map_chunk(c, c, tiles_of(c))
            with pe.Fori(1, TURNS) as turn:
                for s in range(SLOTS):
                    map_chunk(turn * SLOTS + s, s, QT)
            map_chunk(CHUNKS - 1, 0, QT)


_INS = ['x', 'src', 'edge_attr_128', 'L0_gnn_W1', 'L0_gnn_b1', 'L0_gnn_W2', 'L0_gnn_b2']


def kernel(**inputs):
    import numpy as _np
    import concourse.bacc as _bacc
    from concourse import mybir as _mybir
    from concourse.bass_utils import run_bass_kernel_spmd as _run

    nc = _bacc.Bacc("TRN2", target_bir_lowering=False, num_devices=1)
    arrays, args = {}, []
    for name in _INS:
        a = _np.ascontiguousarray(inputs[name])
        arrays[f"in_{name}_dram"] = a
        args.append(nc.dram_tensor(f"in_{name}_dram", a.shape, _mybir.dt.from_np(a.dtype), kind="ExternalInput").ap())
    args.append(nc.dram_tensor("out_0_dram", inputs["x"].shape, _mybir.dt.float32, kind="ExternalOutput").ap())
    bass_segment_sum_resnorm_kernel(nc, *args)
    r = _run(nc, [arrays], core_ids=[0])
    return r.results[0]["out_0_dram"]
```

```python
import concourse.bass as bass
from concourse import mybir
from contextlib import ExitStack


def bass_segment_sum_resnorm_kernel(nc, x, src, edge_attr, w1, b1, w2, b2, out):
    f32, i32, bf16 = mybir.dt.float32, mybir.dt.int32, mybir.dt.bfloat16
    ALU = mybir.AluOpType
    ACT = mybir.ActivationFunctionType

    P = 128
    NODES, D = x.shape
    EDGES = edge_attr.shape[0]
    HID = w1.shape[1]
    EPS = 1e-5
    DMA = 16

    GT = 3
    GROUPS = 8
    U = GT * GROUPS
    LOADS = 4
    LT = U // LOADS
    BLOCKS = EDGES // (P * U)
    COLS = BLOCKS * U
    STEPS = BLOCKS - 3
    DIRECT_AT = STEPS * U
    DIRECT = COLS - DIRECT_AT
    DU = 6
    PASS = DIRECT // DU
    PASSES = 5
    SHARE = NODES // PASSES
    DIRECT_COLS = [(0, 417), (417, 834), (834, SHARE)]
    REST = EDGES - P * COLS
    RT = -(-REST // P)
    LAST = REST - P * (RT - 1)
    REST_GROUPS = [(0, GT), (GT, RT)]
    E = len(REST_GROUPS)
    assert GT < RT <= 2 * GT and DIRECT % DU == 0 and NODES % PASSES == 0

    TABLES = 4
    REST_TABLES = [0, 0, 0, 1]
    FIRST_TABLES = [0, 1, 0, 1] + [(2, 0, 1)[u % 3] for u in range(U - 5)] + [3]
    LOOP_TABLES = [u % TABLES for u in range(U)]
    END_TABLES = [u % (TABLES - 1) for u in range(U)]
    ROWS = NODES + P
    SPLIT = 64
    assert ROWS <= SPLIT * 256 and U % (2 * LOADS) == 0 and len(REST_TABLES) == RT

    DW = D + 1
    NT = NODES // P
    NREST = NODES - P * NT
    QT = 4
    SLOTS = 4
    assert NT % (QT * SLOTS) == 0 and NT == (PASSES - 1) * PASS and PASSES * PASS == STEPS - 4 and BLOCKS % 8 == 3 and D == P and HID == 2 * P

    TURNS = NT // (QT * SLOTS)
    CHUNKS = NT // QT + 1
    part_loads = DMA * (TABLES - 1)

    def tiles_of(c):
        return 1 if c == CHUNKS - 1 else QT

    before = [(REST_TABLES + FIRST_TABLES).count(r) for r in range(TABLES)]
    in_step = [LOOP_TABLES.count(r) for r in range(TABLES)]
    before_end = [before[r] + (STEPS - 2) * in_step[r] for r in range(TABLES)]
    table_total = [before_end[r] + END_TABLES.count(r) for r in range(TABLES)]

    FOLDS = {STEPS - 3: range(0, 5), STEPS - 2: range(5, 9), STEPS - 1: range(9, CHUNKS)}
    assert CHUNKS == 13

    edges_v = edge_attr[0:P * COLS, :].rearrange("(p c) f -> p c f", p=P)
    src_v = src[0:P * COLS].rearrange("(p c) -> p c", p=P)
    x_v = x[0:P * NT, :].rearrange("(p n) f -> p n f", p=P)
    out_v = out[0:P * NT, :].rearrange("(p n) f -> p n f", p=P)
    tables = [nc.dram_tensor(f"table{r}", (ROWS, D), f32, kind="Internal").ap() for r in range(TABLES)]
    tables_v = [t[0:P * NT, :].rearrange("(p n) f -> p n f", p=P) for t in tables]
    ZP = 6
    ZW = ROWS // ZP
    assert ROWS % ZP == 0 and ZP % 2 == 0 and (ROWS * D) // P == ROWS

    with ExitStack() as ctx:
        ctx.enter_context(nc.allow_non_contiguous_dma(reason="b1 as a column, src pieces"))

        def sb(name, shape, dt):
            return ctx.enter_context(nc.sbuf_tensor(name, shape, dt))

        def pb(name):
            return ctx.enter_context(nc.psum_tensor(name, [P, 512], f32))

        def sem(name):
            return ctx.enter_context(nc.semaphore(name))

        src_f = sb("src_f", [P, U + COLS], f32)
        direct_t = sb("direct_t", [P, P * (NT + 1)], f32)
        WH = (BLOCKS + 1) * U
        widths = [WH, WH, WH, ZW]
        starts = [sum(widths[:i]) for i in range(len(widths) + 1)]
        assert starts[-1] <= NODES
        hilo, src_hi, src_i, zeros = (direct_t[:, a:b] for a, b in zip(starts, starts[1:]))
        hilo = hilo.bitcast(bf16).rearrange("p (b h u) -> p b h u", h=2, u=U)
        src_hi = src_hi.bitcast(i32)
        src_i = src_i.bitcast(i32)
        hilo_t = sb("hilo_t", [2 * U, BLOCKS + 1, P], bf16)
        pick_1 = sb("pick_1", [2 * U, U], bf16)
        pick = sb("pick", [2 * U, U, P], bf16)
        data = sb("data", [P, U, DW], f32)
        data_rest = sb("data_rest", [P, RT, DW], f32)
        same = sb("same", [P, 2, GT, P], f32)
        sums = sb("sums", [P, GROUPS + E, GT, DW], f32)
        flag = sb("flag", [P, 2, GT], f32)
        index = sb("index", [P, U + E * GT], i32)
        spare_i = sb("spare_i", [P, 1], i32)
        spare_f = sb("spare_f", [P, 1], f32)
        weight_i = sb("weight_i", [P, 1], i32)
        limit_i = sb("limit_i", [P, 1], i32)
        ident = sb("ident", [P, P], f32)
        ident_b = sb("ident_b", [P, P], bf16)
        w1_sb = sb("w1_sb", [P, 2, HID], f32)
        w2_sb = sb("w2_sb", [P, 2, D], f32)
        b1_sb = sb("b1_sb", [P, 2], f32)
        b2_sb = sb("b2_sb", [1, D], f32)
        w1_t = sb("w1_t", [P, 4, P], f32)
        wab = sb("wab", [P, 2, D], f32)
        bias = sb("bias", [1, D], f32)
        ones = sb("ones", [1, P], f32)
        ones_col = sb("ones_col", [P, 1], f32)
        x_tile = sb("x_tile", [P, D], f32)
        x_rest = sb("x_rest", [P, D], f32)
        x_t = sb("x_t", [P, P], f32)
        y0 = sb("y0", [P, NT + 1, D], f32)
        late = sb("late", [P, (NT + 1) * D + (TABLES - 1) * SLOTS * QT * D + SLOTS * QT * D], f32)
        direct = late[:, 0:3 * DIRECT * D // 2].bitcast(bf16).rearrange("p (h t f) -> p h t f", h=3, f=D)
        early = late[:, 0:(NT + 1) * D].rearrange("p (n f) -> p n f", f=D)
        PW = SLOTS * QT * D
        part = [late[:, (NT + 1) * D + r * PW:(NT + 1) * D + (r + 1) * PW].rearrange(
            "p (s n f) -> p s n f", s=SLOTS, f=D) for r in range(TABLES - 1)]
        z = late[:, (NT + 1) * D + 3 * PW:(NT + 1) * D + 4 * PW].rearrange("p (s n f) -> p s n f", s=SLOTS, f=D)
        agg_t = sb("agg_t", [P, 2, QT * P], f32)
        direct_raw = sb("direct_raw", [P, DU, D], f32)
        minus_src = sb("minus_src", [P, DIRECT], f32)
        node_f = sb("node_f", [P, SHARE], f32)
        distance = sb("distance", [P, 2, SHARE], bf16)
        node_i = distance[:, :, :].rearrange("p a b -> p (a b)").bitcast(i32)
        onehot = sb("onehot", [P, 2, SHARE], bf16)
        zeros_b = sb("zeros_b", [P, 417], bf16)
        stats = sb("stats", [P, QT, 6], f32)
        mv = sb("mv", [P, SLOTS, QT, 2], f32)
        std = sb("std", [P, SLOTS, QT], f32)
        rstd = sb("rstd", [P, SLOTS, QT], f32)
        shift = sb("shift", [P, SLOTS, QT], f32)
        eps = sb("eps", [P, 1], f32)

        p_src = [pb("p_src0"), pb("p_src1")]
        p_sum = [pb("p_sum0"), pb("p_sum1")]
        p_prep = [pb("p_prep0"), pb("p_prep1")]
        p_xt = pb("p_xt")
        p_y = pb("p_y")
        p_direct = [p_prep[0], p_prep[1], p_xt]
        weight = weight_i[:, :].bitcast(f32)
        limit = limit_i[:, :].bitcast(f32)

        src_loaded = sem("src_loaded")
        rest_loaded = sem("rest_loaded")
        weights_loaded = sem("weights_loaded")
        x_rest_loaded = sem("x_rest_loaded")
        x_loaded = sem("x_loaded")
        data_loaded = [sem(f"data_loaded{q}") for q in range(LOADS)]
        table_zeroed = [[sem(f"table_zeroed{r}_{i}") for i in range(2)] for r in range(TABLES)]
        zeros_ready = sem("zeros_ready")
        fills_ready = sem("fills_ready")
        consts_ready = sem("consts_ready")
        ident_ready = sem("ident_ready")
        data_rest_loaded = sem("data_rest_loaded")
        pool_fills = sem("pool_fills")
        pool_step = sem("pool_step")
        pick_ready = sem("pick_ready")
        dve_step = sem("dve_step")
        hilo_ready = sem("hilo_ready")
        weights_ready = sem("weights_ready")
        prep_done = sem("prep_done")
        prep_copied = sem("prep_copied")
        src_spread = sem("src_spread")
        same_ready = sem("same_ready")
        summed = sem("summed")
        sums_ready = sem("sums_ready")
        flag_ready = sem("flag_ready")
        index_ready = sem("index_ready")
        landed = [sem(f"landed{r}") for r in range(TABLES)]
        w1_t_done = sem("w1_t_done")
        w1_t_ready = sem("w1_t_ready")
        wab_done = sem("wab_done")
        wab_ready = sem("wab_ready")
        x_t_done = sem("x_t_done")
        x_t_ready = sem("x_t_ready")
        y_done = sem("y_done")
        y0_ready = sem("y0_ready")
        raw_loaded = sem("raw_loaded")
        split_step = sem("split_step")
        minus_src_ready = sem("minus_src_ready")
        node_ready = sem("node_ready")
        zeros_b_ready = sem("zeros_b_ready")
        distance_ready = sem("distance_ready")
        onehot_ready = sem("onehot_ready")
        direct_done = sem("direct_done")
        pass_done = sem("pass_done")
        pass_copied = sem("pass_copied")
        part_loaded = [sem(f"part_loaded{s}") for s in range(SLOTS)]
        early_loaded = sem("early_loaded")
        two_added = sem("two_added")
        half_added = sem("half_added")
        agg_ready = sem("agg_ready")
        agg_t_done = sem("agg_t_done")
        agg_t_ready = sem("agg_t_ready")
        map_done = sem("map_done")
        z_ready = sem("z_ready")
        stats_ready = sem("stats_ready")
        rstd_ready = sem("rstd_ready")
        moments_ready = sem("moments_ready")
        std_ready = sem("std_ready")
        scale_ready = sem("scale_ready")
        result_ready = sem("result_ready")
        stored = sem("stored")

        block = ctx.enter_context(nc.Block())

        @block.sync
        def _(sp):
            sp.dma_start(src_i[:, U:U + COLS], src_v).then_inc(src_loaded, DMA)
            sp.wait_ge(pool_fills, 1)
            sp.dma_start(src_i[:, 0:RT - 1],
                         src[P * COLS:EDGES - LAST].rearrange("(p c) -> p c", p=P)).then_inc(rest_loaded, DMA)
            sp.dma_start(src_i[0:LAST, RT - 1:RT],
                         src[EDGES - LAST:EDGES].rearrange("(p c) -> p c", p=LAST)).then_inc(rest_loaded, DMA)
            sp.wait_ge(fills_ready, 1)
            sp.dma_start(data_rest[:, 0:RT - 1, 0:D],
                         edge_attr[P * COLS:EDGES - LAST, :].rearrange("(p c) f -> p c f", p=P)
                         ).then_inc(data_rest_loaded, DMA)
            sp.dma_start(data_rest[0:LAST, RT - 1, 0:D],
                         edge_attr[EDGES - LAST:EDGES, :]).then_inc(data_rest_loaded, DMA)
            sp.wait_ge(zeros_ready, 1)

            def zero(r, piece):
                if piece >= 2:
                    sp.wait_ge(table_zeroed[r][piece % 2], DMA * (piece // 2))
                sp.dma_start(tables[r].rearrange("a f -> (a f)").rearrange("(p b c) -> p b c", p=P, b=ZP)[:, piece, :],
                             zeros[:, :]).then_inc(table_zeroed[r][piece % 2], DMA)

            def first_load(q):
                sp.dma_start(data[:, q * LT:(q + 1) * LT, 0:D],
                             edges_v[:, q * LT:(q + 1) * LT, :]).then_inc(data_loaded[q], DMA)

            for piece in range(ZP):
                zero(0, piece)
            first_load(0)
            for piece in range(ZP):
                zero(1, piece)
                if piece % 2 and piece // 2 + 1 < LOADS:
                    first_load(piece // 2 + 1)
            sp.dma_start(w1_sb[:, :, :], w1.rearrange("(k p) h -> p k h", p=P)).then_inc(weights_loaded, DMA)
            sp.dma_start(w2_sb[:, :, :], w2.rearrange("(k p) h -> p k h", p=P)).then_inc(weights_loaded, DMA)
            sp.dma_start(b1_sb[:, :], b1.rearrange("(k p) -> p k", p=P)).then_inc(weights_loaded, DMA)
            sp.dma_start(b2_sb[:, :], b2.rearrange("(o f) -> o f", o=1)).then_inc(weights_loaded, DMA)
            sp.dma_start(x_rest[0:NREST, :], x[P * NT:NODES, :]).then_inc(x_rest_loaded, DMA)
            sp.dma_start(x_tile[:, :], x_v[:, 0, :]).then_inc(x_loaded, DMA)
            for r in range(2, TABLES):
                for piece in range(ZP):
                    zero(r, piece)

            def load_edges(step):
                for q in range(LOADS):
                    sp.wait_ge(summed, step * GROUPS + (E + (q + 1) * GROUPS // LOADS))
                    sp.dma_start(data[:, q * LT:(q + 1) * LT, 0:D],
                                 edges_v[:, bass.ds(step * U + (U + q * LT), LT), :]
                                 ).then_inc(data_loaded[q], DMA)

            def load_x(step):
                sp.wait_ge(y0_ready, step + 1)
                sp.dma_start(x_tile[:, :], x_v[:, bass.ds(step, 1), :].rearrange("p n f -> p (n f)")
                             ).then_inc(x_loaded, DMA)

            sp.dma_start(direct_raw[:, :, :], edges_v[:, DIRECT_AT:DIRECT_AT + DU, :]).then_inc(raw_loaded, DMA)
            load_edges(0)
            with sp.Fori(1, PASS) as step:
                sp.wait_ge(split_step, step * 4)
                sp.dma_start(direct_raw[:, :, :], edges_v[:, bass.ds(step * DU + DIRECT_AT, DU), :]
                             ).then_inc(raw_loaded, DMA)
                load_edges(step)
                load_x(step)
            with sp.Fori(PASS, NT) as step:
                load_edges(step)
                load_x(step)
            with sp.Fori(NT, STEPS - 1) as step:
                load_edges(step)

            out_of_use = TABLES - 1
            sp.wait_ge(direct_done, PASSES * DIRECT)
            sp.wait_ge(landed[out_of_use], DMA * table_total[out_of_use])
            sp.dma_start(early[:, NT, :], tables[out_of_use][P * NT:P * NT + P, :]).then_inc(early_loaded, DMA)
            for q in range(NT // QT):
                sp.wait_ge(landed[0], DMA * (before_end[0] + q // 2))
                sp.dma_start(early[:, q * QT:(q + 1) * QT, :], tables_v[out_of_use][:, q * QT:(q + 1) * QT, :]
                             ).then_inc(early_loaded, DMA)

            for r in range(TABLES - 1):
                sp.wait_ge(landed[r], DMA * table_total[r])
            def load_chunk(c, s):
                for r in range(TABLES - 1):
                    sp.dma_start(part[r][:, s, :, :], tables_v[r][:, bass.ds(c * QT, QT), :]
                                 ).then_inc(part_loaded[s], DMA)

            for c in range(SLOTS):
                load_chunk(c, c)
            with sp.Fori(1, TURNS) as turn:
                for s in range(SLOTS):
                    c = turn * SLOTS + s
                    sp.wait_ge(agg_t_done, c - (SLOTS - 1))
                    load_chunk(c, s)
            sp.wait_ge(agg_t_done, CHUNKS - SLOTS)
            for r in range(TABLES - 1):
                sp.dma_start(part[r][:, 0, 0, :], tables[r][P * NT:P * NT + P, :]).then_inc(part_loaded[0], DMA)

        @block.gpsimd
        def _(pool):
            nc.gpsimd.iota(src_i[:, RT - 1:U], [[0, U - RT + 1]], base=NODES, channel_multiplier=1
                           ).then_inc(pool_fills, 1)
            nc.gpsimd.memset(ident_b[:, :], 0.0)
            nc.gpsimd.memset(pick_1[:, :], 0.0)
            nc.gpsimd.memset(ident[:, :], 0.0).then_inc(pool_step, 1)
            pool.wait_ge(pool_step, 1)
            nc.gpsimd.affine_select(out=pick_1[:, :], in_=pick_1[:, :], compare_op=ALU.not_equal, fill=1.0,
                                    base=0, pattern=[[-1, U]], channel_multiplier=1).then_inc(pool_step, 1)
            pool.wait_ge(pool_step, 2)
            nc.gpsimd.affine_select(out=pick_1[:, :], in_=pick_1[:, :], compare_op=ALU.not_equal, fill=1.0,
                                    base=-U, pattern=[[-1, U]], channel_multiplier=1).then_inc(pool_step, 1)
            nc.gpsimd.affine_select(out=ident_b[:, :], in_=ident_b[:, :], compare_op=ALU.not_equal, fill=1.0,
                                    base=0, pattern=[[-1, P]], channel_multiplier=1)
            nc.gpsimd.iota(spare_i[:, :], [[0, 1]], base=NODES, channel_multiplier=1)
            nc.gpsimd.iota(weight_i[:, :], [[0, 1]], base=(127 + 60) << 23, channel_multiplier=-(1 << 23))
            nc.gpsimd.iota(limit_i[:, :], [[0, 1]], base=((127 + 61) << 23) + (1 << 21),
                           channel_multiplier=-(1 << 23)).then_inc(consts_ready, 1)
            nc.gpsimd.affine_select(out=ident[:, :], in_=ident[:, :], compare_op=ALU.not_equal, fill=1.0,
                                    base=0, pattern=[[-1, P]], channel_multiplier=1).then_inc(ident_ready, 1)
            nc.gpsimd.iota(node_i[:, :], [[1, SHARE]], base=0, channel_multiplier=0).then_inc(node_ready, 1)

            def scatter(slot, r, done, group_count):
                for i in range(2):
                    pool.wait_ge(table_zeroed[r][i], DMA * ZP // 2)
                if group_count is not None:
                    pool.wait_ge(index_ready, group_count)
                if not (isinstance(done, int) and done == 0):
                    pool.wait_ge(landed[r], done)
                pool.indirect_dma_start(
                    out=tables[r][:, :], out_offset=bass.IndirectOffsetOnAxis(ap=index[:, slot:slot + 1], axis=0),
                    in_=sums[:, slot // GT, slot % GT, 0:D], in_offset=None,
                    compute_op=ALU.add).then_inc(landed[r], DMA)

            for t, r in enumerate(REST_TABLES):
                scatter(U + t, r, DMA * REST_TABLES[:t].count(r), t // GT + 1 if t % GT == 0 else None)
            for u, r in enumerate(FIRST_TABLES):
                scatter(u, r, DMA * (REST_TABLES + FIRST_TABLES[:u]).count(r),
                        E + u // GT + 1 if u % GT == 0 else None)

            landed_count = [pool.alloc_register(f"landed_count{r}") for r in range(TABLES)]
            index_count = pool.alloc_register("index_count")
            for r in range(TABLES):
                pool.reg_mov(landed_count[r], DMA * (before[r] - 1))
            pool.reg_mov(index_count, E + GROUPS)
            assert all(n > 0 for n in before)
            with pool.Fori(1, STEPS - 1) as step:
                for u, r in enumerate(LOOP_TABLES):
                    pool.reg_add(landed_count[r], landed_count[r], DMA)
                    if u % GT == 0:
                        pool.reg_add(index_count, index_count, 1)
                    scatter(u, r, landed_count[r], index_count if u % GT == 0 else None)
            for u, r in enumerate(END_TABLES):
                scatter(u, r, DMA * (before_end[r] + END_TABLES[:u].count(r)),
                        E + (STEPS - 1) * GROUPS + u // GT + 1 if u % GT == 0 else None)

            pool.wait_ge(early_loaded, DMA * CHUNKS)
            for c in range(CHUNKS):
                s, n = c % SLOTS, tiles_of(c)
                pool.wait_ge(part_loaded[s], part_loads * (c // SLOTS + 1))
                nc.gpsimd.tensor_tensor(out=part[1][:, s, 0:n, :], in0=part[1][:, s, 0:n, :],
                                        in1=part[2][:, s, 0:n, :], op=ALU.add).then_inc(two_added, 1)
                pool.wait_ge(two_added, c + 1)
                nc.gpsimd.tensor_tensor(out=part[1][:, s, 0:n, :], in0=part[1][:, s, 0:n, :],
                                        in1=early[:, c * QT:c * QT + n, :], op=ALU.add).then_inc(half_added, 1)

        @block.scalar
        def _(act):
            act.wait_ge(fills_ready, 2)
            nc.scalar.activation(std[:, 0, 0:1], eps[:, :], ACT.Sqrt)
            act.wait_ge(pool_step, 3)
            nc.scalar.copy(pick[:, :, :], pick_1[:, :].unsqueeze(2).to_broadcast([2 * U, U, P])).then_inc(pick_ready, 1)

            def copy_prep(first, i, count):
                act.wait_ge(prep_done, count)
                nc.scalar.copy(hilo_t[:, bass.ds(first, 4), :],
                               p_prep[i][0:2 * U, :].rearrange("p (b c) -> p b c", c=P)).then_inc(prep_copied, 1)

            copy_prep(0, 0, 1)

            def take_sums(slot, bank, tiles, count):
                act.wait_ge(summed, count)
                nc.scalar.copy(sums[:, slot, 0:tiles, :], p_sum[bank][:, 0:tiles * DW].rearrange(
                    "p (t c) -> p t c", c=DW)).then_inc(sums_ready, 1)

            for e, (t0, t1) in enumerate(REST_GROUPS):
                take_sums(GROUPS + e, e, t1 - t0, e + 1)
            for k in range(GROUPS):
                take_sums(k, k % 2, GT, E + k + 1)

            with act.Fori(0, BLOCKS // 8) as turn:
                for i in range(2):
                    copy_prep(turn * 8 + (4 + 4 * i), 1 - i, turn * 2 + (i + 2))

            act.wait_ge(w1_t_done, 1)
            nc.scalar.copy(w1_t[:, :, :], p_xt[:, :].rearrange("p (b c) -> p b c", c=P)).then_inc(w1_t_ready, 1)
            act.wait_ge(wab_done, 1)
            nc.scalar.copy(wab[:, :, :], p_y[:, 0:2 * D].rearrange("p (b c) -> p b c", c=D))
            nc.scalar.copy(bias[:, :], p_y[0:1, 2 * D:3 * D]).then_inc(wab_ready, 1)

            def copy_x_t(n):
                act.wait_ge(x_t_done, n + 1)
                act.wait_ge(y_done, n)
                nc.scalar.copy(x_t[:, :], p_y[:, D:D + P]).then_inc(x_t_ready, 1)

            copy_x_t(0)

            def select(count, tile, i):
                nc.scalar.activation(distance[:, i % 2, :], node_f[:, :], ACT.Abs,
                                     bias=minus_src[:, bass.ds(tile, 1)]).then_inc(distance_ready, 1)
                act.wait_ge(distance_ready, count + 1)
                if not (isinstance(count, int) and count < 2):
                    act.wait_ge(direct_done, count - 1)
                nc.scalar.activation(onehot[:, i % 2, :], distance[:, i % 2, :], ACT.Relu, bias=ones_col[:, :],
                                     scale=-1.0).then_inc(onehot_ready, 1)

            def copy_pass(q):
                act.wait_ge(pass_done, q + 1)
                for (c0, c1), bank in zip(DIRECT_COLS, p_direct):
                    last = nc.scalar.copy(direct_t[:, bass.ds(q * SHARE + c0, c1 - c0)], bank[:, 0:c1 - c0])
                last.then_inc(pass_copied, 1)

            def steps(step, slot_landed, node, turn=None):
                for k in range(GROUPS):
                    for u in range(k * GT, (k + 1) * GT):
                        act.wait_ge(*slot_landed(u))
                    take_sums(k, k % 2, GT, step * GROUPS + (E + k + 1))
                    if node and k == 1:
                        copy_x_t(step)
                    if turn is not None and 1 <= k <= DU:
                        select((step - 1) * DU + (k - 1), turn * DU + (k - 1), k - 1)

            def after_first(u):
                r = FIRST_TABLES[u]
                return landed[r], DMA * (REST_TABLES + FIRST_TABLES[:u + 1]).count(r)

            def after(step):
                def slot_landed(u):
                    r = LOOP_TABLES[u]
                    return landed[r], (step - 2) * (DMA * in_step[r]) + DMA * (
                        before[r] + LOOP_TABLES[:u + 1].count(r))
                return slot_landed

            act.wait_ge(minus_src_ready, 1)
            steps(1, after_first, True, 0)
            with act.Fori(2, PASS + 1) as step:
                steps(step, after(step), True, step - 1)
            copy_pass(0)
            with act.Fori(1, PASSES - 1) as q:
                act.wait_ge(minus_src_ready, q + 1)
                with act.Fori(0, PASS) as turn:
                    step = q * PASS + turn + 1
                    steps(step, after(step), True, turn)
                copy_pass(q)
            act.wait_ge(minus_src_ready, PASSES)
            with act.Fori(0, PASS) as turn:
                step = turn + ((PASSES - 1) * PASS + 1)
                steps(step, after(step), False, turn)
            copy_pass(PASSES - 1)
            for step in range(PASSES * PASS + 1, STEPS):
                steps(step, after(step), False)

            def copy_agg_t(s, n, count):
                act.wait_ge(agg_t_done, count + 1)
                if not (isinstance(count, int) and count < 2):
                    act.wait_ge(map_done, count - 1)
                nc.scalar.copy(agg_t[:, s % 2, 0:n * P], p_prep[s % 2][:, 0:n * P]).then_inc(agg_t_ready, 1)

            def root(s, n, count):
                act.wait_ge(moments_ready, count + 1)
                nc.scalar.activation(std[:, s, 0:n], mv[:, s, 0:n, 1], ACT.Sqrt, bias=eps[:, :]
                                     ).then_inc(std_ready, 1)

            def normalise(c, s, n, tile):
                act.wait_ge(scale_ready, c + 1)
                for t in range(n):
                    last = nc.scalar.activation(y0[:, bass.ds(tile + t, 1), :].rearrange("p n f -> p (n f)"),
                                                z[:, s, t, :], ACT.Identity,
                                                bias=shift[:, s, t:t + 1], scale=rstd[:, s, t:t + 1])
                last.then_inc(result_ready, 1)

            def store_chunk(c):
                act.wait_ge(result_ready, c + 1)
                act.dma_start(out_v[:, bass.ds(c * QT, QT), :], y0[:, bass.ds(c * QT, QT), :]
                              ).then_inc(stored, DMA)

            for c in range(SLOTS):
                copy_agg_t(c, tiles_of(c), c)
                if c >= 1:
                    root(c - 1, tiles_of(c - 1), c - 1)
                if c >= 2:
                    normalise(c - 2, c - 2, tiles_of(c - 2), (c - 2) * QT)
                if c >= 3:
                    store_chunk(c - 3)
            with act.Fori(1, TURNS) as turn:
                for s in range(SLOTS):
                    c = turn * SLOTS + s
                    copy_agg_t(s, QT, c)
                    root((s - 1) % SLOTS, QT, c - 1)
                    normalise(c - 2, (s - 2) % SLOTS, QT, (c - 2) * QT)
                    store_chunk(c - 3)
            copy_agg_t(0, 1, CHUNKS - 1)
            root(SLOTS - 1, QT, CHUNKS - 2)
            normalise(CHUNKS - 3, SLOTS - 2, QT, NT - 2 * QT)
            store_chunk(CHUNKS - 4)
            root(0, 1, CHUNKS - 1)
            normalise(CHUNKS - 2, SLOTS - 1, QT, NT - QT)
            store_chunk(CHUNKS - 3)
            normalise(CHUNKS - 1, 0, 1, NT)
            store_chunk(CHUNKS - 2)
            act.wait_ge(result_ready, CHUNKS)
            act.dma_start(out[P * NT:NODES, :], y0[0:NREST, NT, :]).then_inc(stored, DMA)
            act.wait_ge(stored, DMA * CHUNKS)

        @block.vector
        def _(dve):
            nc.vector.memset(zeros[:, :], 0.0).then_inc(zeros_ready, 1)
            nc.vector.memset(data_rest[:, RT - 1, :], 0.0)
            nc.vector.memset(x_rest[:, :], 0.0).then_inc(fills_ready, 1)
            nc.vector.memset(ones[:, :], 1.0)
            nc.vector.memset(ones_col[:, :], 1.0)
            nc.vector.memset(direct_t[:, NODES:], 0.0)
            nc.vector.memset(zeros_b[:, :], 0.0).then_inc(zeros_b_ready, 1)
            nc.vector.memset(eps[:, :], EPS).then_inc(fills_ready, 1)
            dve.wait_ge(src_loaded, DMA)
            dve.wait_ge(rest_loaded, 2 * DMA)
            for i, (b0, b1_) in enumerate(((0, 4), (4, BLOCKS + 1))):
                c0, c1 = b0 * U, b1_ * U
                hi = src_hi[:, c0:c1]
                nc.vector.tensor_scalar(hi, src_i[:, c0:c1], -SPLIT, None, ALU.bitwise_and).then_inc(dve_step, 1)
                nc.vector.tensor_copy(src_f[:, c0:c1], src_i[:, c0:c1])
                dve.wait_ge(dve_step, i + 1)
                hi = hi.rearrange("p (b w) -> p b w", w=U)
                nc.vector.tensor_copy(hilo[:, b0:b1_, 0, :], hi)
                nc.vector.tensor_tensor(hilo[:, b0:b1_, 1, :], src_i[:, c0:c1].rearrange("p (b w) -> p b w", w=U),
                                        hi, ALU.subtract).then_inc(hilo_ready, 1)
                if i == 0:
                    dve.wait_ge(consts_ready, 1)
                    nc.vector.tensor_copy(spare_f[:, :], spare_i[:, :])
                    nc.vector.tensor_copy(data_rest[:, :, D:DW], weight.unsqueeze(1).to_broadcast([P, RT, 1]))
                    nc.vector.tensor_copy(data[:, :, D:DW], weight.unsqueeze(1).to_broadcast([P, U, 1])
                                          ).then_inc(weights_ready, 1)
            dve.wait_ge(weights_ready, 1)
            dve.wait_ge(hilo_ready, 2)
            dve.wait_ge(node_ready, 1)
            nc.vector.tensor_copy(node_f[:, :], node_i[:, :])
            nc.vector.tensor_scalar(minus_src[:, :], src_f[:, U + DIRECT_AT:U + COLS], -1.0, None, ALU.mult
                                    ).then_inc(minus_src_ready, 1)

            def compare(k, tiles, col, group):
                dve.wait_ge(src_spread, group + 1)
                if not (isinstance(group, int) and group < 2):
                    dve.wait_ge(summed, group - 1)
                nc.vector.tensor_tensor(
                    same[:, k % 2, 0:tiles, :], p_src[k % 2][:, 0:tiles * P].rearrange("p (t c) -> p t c", c=P),
                    src_f[:, bass.ds(col, tiles)].unsqueeze(2).to_broadcast([P, tiles, P]), ALU.is_equal
                ).then_inc(same_ready, 1)

            def rows(k, tiles, col, group):
                dve.wait_ge(sums_ready, group + 1)
                nc.vector.tensor_scalar(flag[:, k % 2, 0:tiles], sums[:, k, 0:tiles, D], limit, spare_f[:, :],
                                        ALU.is_gt, ALU.mult).then_inc(flag_ready, 1)
                dve.wait_ge(flag_ready, group + 1)
                nc.vector.tensor_tensor(index[:, k * GT:k * GT + tiles], flag[:, k % 2, 0:tiles],
                                        src_f[:, bass.ds(col, tiles)], ALU.max).then_inc(index_ready, 1)

            def add_y0(n, tile, x_used):
                dve.wait_ge(y_done, n + 1)
                nc.vector.tensor_tensor(y0[:, bass.ds(tile, 1), :].rearrange("p n f -> p (n f)"),
                                        p_y[:, 0:D], x_used[:, :], ALU.add).then_inc(y0_ready, 1)

            for e, (t0, t1) in enumerate(REST_GROUPS):
                compare(GROUPS + e, t1 - t0, t0, e)
                if e:
                    rows(GROUPS + e - 1, GT, 0, e - 1)
            rows(GROUPS + E - 1, RT - GT, GT, E - 1)

            def split(i, step):
                if i == 0:
                    dve.wait_ge(raw_loaded, step * DMA)
                else:
                    dve.wait_ge(split_step, step * 4 - (4 - i))
                part_of = direct[:, (0, 0, 1, 2)[i], bass.ds(step * DU - DU, DU), :]
                if i % 2 == 0:
                    nc.vector.tensor_scalar(part_of, direct_raw[:, :, :], 1.0, None, ALU.mult).then_inc(split_step, 1)
                elif i == 1:
                    nc.vector.tensor_tensor(direct_raw[:, :, :], direct_raw[:, :, :], part_of, ALU.subtract
                                            ).then_inc(split_step, 1)
                else:
                    nc.vector.tensor_tensor(part_of, direct_raw[:, :, :], direct[:, 1, bass.ds(step * DU - DU, DU), :],
                                            ALU.subtract).then_inc(split_step, 1)

            def next_share(q):
                dve.wait_ge(distance_ready, (q + 1) * DIRECT)
                nc.vector.tensor_scalar(minus_src[:, :], minus_src[:, :], float(SHARE), None, ALU.add
                                        ).then_inc(minus_src_ready, 1)

            def add_direct(f):
                n0, n = f * QT, tiles_of(f)
                dve.wait_ge(y_done, NT + 1 + f + 1)
                nc.vector.tensor_tensor(y0[:, n0:n0 + n, :], y0[:, n0:n0 + n, :], p_y[:, 0:n * D].rearrange(
                    "p (t c) -> p t c", c=D), ALU.add).then_inc(y0_ready, 1)

            def steps(step, node, folds=(), split_next=False):
                for k in range(GROUPS):
                    compare(k, GT, step * U + (U + k * GT), step * GROUPS + (E + k))
                    if k:
                        rows(k - 1, GT, step * U + (U + (k - 1) * GT), step * GROUPS + (E + k - 1))
                    if node and k == 5:
                        add_y0(step, step - 1, x_tile)
                    if split_next and k >= GROUPS - 4:
                        split(k - (GROUPS - 4), step + 1)
                    if 1 <= k <= len(folds):
                        add_direct(folds[k - 1])
                rows(GROUPS - 1, GT, step * U + (U + (GROUPS - 1) * GT), step * GROUPS + (E + GROUPS - 1))

            steps(0, False)
            add_y0(0, NT, x_rest)
            for i in range(4):
                split(i, 1)
            with dve.Fori(1, PASS) as step:
                steps(step, True, (), True)
            steps(PASS, True)
            next_share(0)
            with dve.Fori(1, PASSES - 1) as q:
                with dve.Fori(0, PASS) as turn:
                    steps(q * PASS + turn + 1, True)
                next_share(q)
            with dve.Fori((PASSES - 1) * PASS + 1, PASSES * PASS + 1) as step:
                steps(step, False)
            for step in range(PASSES * PASS + 1, STEPS):
                steps(step, False, FOLDS[step])

            def add_parts(c, s, n, loads):
                dve.wait_ge(part_loaded[s], loads)
                dve.wait_ge(half_added, c + 1)
                nc.vector.tensor_tensor(part[0][:, s, 0:n, :], part[0][:, s, 0:n, :], part[1][:, s, 0:n, :],
                                        ALU.add).then_inc(agg_ready, 1)

            def moments(c, s, n, tile):
                dve.wait_ge(map_done, c + 1)
                if not (isinstance(c, int) and c < SLOTS):
                    dve.wait_ge(result_ready, c - (SLOTS - 1))
                nc.vector.tensor_tensor(z[:, s, 0:n, :], p_src[s % 2][:, 0:n * D].rearrange(
                    "p (t c) -> p t c", c=D), y0[:, bass.ds(tile, n), :], ALU.add).then_inc(z_ready, 1)
                dve.wait_ge(z_ready, c + 1)
                for t in range(n):
                    last = nc.vector.bn_stats(stats[:, t, :], z[:, s, t, :])
                last.then_inc(stats_ready, 1)

            def aggregate(c, s, n):
                for t in range(n):
                    last = nc.vector.bn_aggr(mv[:, s, t, :], stats[:, t, :])
                last.then_inc(moments_ready, 1)

            def scales(c, s, n):
                dve.wait_ge(std_ready, c + 1)
                dve.wait_ge(stats_ready, min(c + 2, CHUNKS) if isinstance(c, int) else c + 2)
                nc.vector.reciprocal(rstd[:, s, 0:n], std[:, s, 0:n]).then_inc(rstd_ready, 1)
                if not (isinstance(c, int) and c + 1 == CHUNKS):
                    aggregate(c + 1, (s + 1) % SLOTS, tiles_of(c + 1) if isinstance(c, int) else QT)
                dve.wait_ge(rstd_ready, c + 1)
                nc.vector.scalar_tensor_tensor(shift[:, s, 0:n], mv[:, s, 0:n, 0], -1.0, rstd[:, s, 0:n],
                                               ALU.mult, ALU.mult).then_inc(scale_ready, 1)

            for c in range(SLOTS):
                add_parts(c, c, tiles_of(c), part_loads)
                if c >= 1:
                    moments(c - 1, c - 1, tiles_of(c - 1), (c - 1) * QT)
                if c == 1:
                    dve.wait_ge(stats_ready, 1)
                    aggregate(0, 0, tiles_of(0))
                if c >= 2:
                    scales(c - 2, c - 2, tiles_of(c - 2))
            with dve.Fori(1, TURNS) as turn:
                for s in range(SLOTS):
                    c = turn * SLOTS + s
                    add_parts(c, s, QT, turn * part_loads + part_loads)
                    moments(c - 1, (s - 1) % SLOTS, QT, (c - 1) * QT)
                    scales(c - 2, (s - 2) % SLOTS, QT)
            add_parts(CHUNKS - 1, 0, 1, part_loads * (TURNS + 1))
            moments(CHUNKS - 2, SLOTS - 1, QT, NT - QT)
            scales(CHUNKS - 3, SLOTS - 2, QT)
            moments(CHUNKS - 1, 0, 1, NT)
            scales(CHUNKS - 2, SLOTS - 1, QT)
            scales(CHUNKS - 1, 0, 1)

        @block.tensor
        def _(pe):
            pe.wait_ge(consts_ready, 1)
            pe.wait_ge(hilo_ready, 1)

            def prepare(first, i):
                for b in range(4):
                    last = nc.tensor.matmul(
                        p_prep[i][0:2 * U, b * P:(b + 1) * P],
                        lhsT=hilo[:, bass.ds(first + b, 1), :, :].rearrange("p b h u -> p (b h u)"),
                        rhs=ident_b[:, :], start=True, stop=True)
                last.then_inc(prep_done, 1)

            prepare(0, 0)
            def turn_x(n, x_used):
                if not isinstance(n, int):
                    pe.wait_ge(y0_ready, n)
                nc.tensor.transpose(p_y[:, D:D + P], x_used[:, :], ident[:, :]).then_inc(x_t_done, 1)

            def map_x(n):
                pe.wait_ge(x_t_ready, n + 1)
                nc.tensor.matmul(p_y[:, 0:D], lhsT=x_t[:, :], rhs=wab[:, 0, :], start=True, stop=False)
                nc.tensor.matmul(p_y[:, 0:D], lhsT=ones[:, :], rhs=bias[:, :], start=False, stop=True
                                 ).then_inc(y_done, 1)

            pe.wait_ge(prep_copied, 1)
            pe.wait_ge(pick_ready, 1)

            def spread(k, tiles, block_at):
                for t in range(tiles):
                    last = nc.tensor.matmul(
                        p_src[k % 2][:, t * P:(t + 1) * P],
                        lhsT=pick[:, k * GT + t, :],
                        rhs=hilo_t[:, bass.ds(block_at, 1), :].rearrange("q b j -> q (b j)"), start=True, stop=True)
                last.then_inc(src_spread, 1)

            def add_up(k, tiles, rows_of, group):
                pe.wait_ge(same_ready, group + 1)
                if not (isinstance(group, int) and group < 2):
                    pe.wait_ge(sums_ready, group - 1)
                for t in range(tiles):
                    last = nc.tensor.matmul(p_sum[k % 2][:, t * DW:(t + 1) * DW], lhsT=same[:, k % 2, t, :],
                                            rhs=rows_of[:, t, :], start=True, stop=True)
                last.then_inc(summed, 1)

            for e, (t0, t1) in enumerate(REST_GROUPS):
                for t in range(t0, t1):
                    last = nc.tensor.matmul(p_src[e][:, (t - t0) * P:(t - t0 + 1) * P], lhsT=pick[:, t, :],
                                            rhs=hilo_t[:, 0, :], start=True, stop=True)
                last.then_inc(src_spread, 1)
            pe.wait_ge(weights_ready, 1)
            pe.wait_ge(data_rest_loaded, 2 * DMA)
            for e, (t0, t1) in enumerate(REST_GROUPS):
                add_up(e, t1 - t0, data_rest[:, t0:t1, :], e)

            def open_pass():
                for (c0, c1), bank in zip(DIRECT_COLS, p_direct):
                    nc.tensor.matmul(bank[:, 0:c1 - c0], lhsT=zeros_b[:, 0:P], rhs=zeros_b[:, 0:c1 - c0],
                                     start=True, stop=False)

            def close_pass():
                for (c0, c1), bank in zip(DIRECT_COLS, p_direct):
                    last = nc.tensor.matmul(bank[:, 0:c1 - c0], lhsT=zeros_b[:, 0:P], rhs=zeros_b[:, 0:c1 - c0],
                                            start=False, stop=True)
                last.then_inc(pass_done, 1)

            def add_direct(count, tile, i):
                pe.wait_ge(onehot_ready, count + 1)
                for h in range(3):
                    for (c0, c1), bank in zip(DIRECT_COLS, p_direct):
                        last = nc.tensor.matmul(
                            bank[:, 0:c1 - c0],
                            lhsT=direct[:, h, bass.ds(tile, 1), :].rearrange("p t f -> p (t f)"),
                            rhs=onehot[:, i % 2, c0:c1], start=False, stop=False)
                last.then_inc(direct_done, 1)

            def map_direct(f):
                pe.wait_ge(y0_ready, NT + 1 + f)
                for t in range(tiles_of(f)):
                    n = f * QT + t
                    of_tile = direct_t[:, n:n + NT * (P - 1) + 1:NT] if n < NT else direct_t[:, P * NT:P * NT + P]
                    last = nc.tensor.matmul(p_y[:, t * D:(t + 1) * D], lhsT=of_tile, rhs=wab[:, 1, :],
                                            start=True, stop=True)
                last.then_inc(y_done, 1)

            def steps(step, node, turn=None, folds=(), split_first=False):
                for k in range(GROUPS):
                    group = step * GROUPS + (E + k)
                    if k == 0:
                        spread(0, GT, step + 1)
                    if k + 1 < GROUPS:
                        spread(k + 1, GT, step + 1)
                    if k % (GROUPS // LOADS) == 0:
                        pe.wait_ge(data_loaded[k // (GROUPS // LOADS)], step * DMA + DMA)
                    add_up(k, GT, data[:, k * GT:(k + 1) * GT, :], group)
                    if node and k == 0:
                        pe.wait_ge(x_loaded, step * DMA)
                        turn_x(step, x_tile)
                    if node and k == 3:
                        map_x(step)
                    if split_first and k == 2:
                        pe.wait_ge(split_step, step * 4)
                    if turn is not None and 2 <= k <= DU + 1:
                        add_direct((step - 1) * DU + (k - 2), turn * DU + (k - 2), k - 2)
                    if k < len(folds):
                        map_direct(folds[k])

            steps(0, False)

            pe.wait_ge(hilo_ready, 2)
            with pe.Fori(0, BLOCKS // 8) as turn:
                for i in range(2):
                    pe.wait_ge(prep_copied, turn * 2 + 1)
                    prepare(turn * 8 + (4 + 4 * i), 1 - i)

            pe.wait_ge(weights_loaded, 4 * DMA)
            pe.wait_ge(ident_ready, 1)
            for k in range(2):
                for h in range(2):
                    last = nc.tensor.transpose(p_xt[:, (2 * k + h) * P:(2 * k + h + 1) * P],
                                               w1_sb[:, k, h * P:(h + 1) * P], ident[:, :])
            last.then_inc(w1_t_done, 1)
            pe.wait_ge(w1_t_ready, 1)
            for k in range(2):
                for h in range(2):
                    nc.tensor.matmul(p_y[:, k * D:(k + 1) * D], lhsT=w1_t[:, 2 * k + h, :], rhs=w2_sb[:, h, :],
                                     start=(h == 0), stop=(h == 1))
            for h in range(2):
                nc.tensor.matmul(p_y[0:1, 2 * D:3 * D], lhsT=b1_sb[:, h:h + 1], rhs=w2_sb[:, h, :],
                                 start=(h == 0), stop=False)
            nc.tensor.matmul(p_y[0:1, 2 * D:3 * D], lhsT=ones[0:1, 0:1], rhs=b2_sb[:, :],
                             start=False, stop=True).then_inc(wab_done, 1)

            pe.wait_ge(wab_ready, 1)
            pe.wait_ge(x_rest_loaded, DMA)
            turn_x(0, x_rest)
            map_x(0)
            pe.wait_ge(prep_copied, BLOCKS // 4 + 1)

            pe.wait_ge(zeros_b_ready, 1)
            open_pass()
            with pe.Fori(1, PASS + 1) as step:
                steps(step, True, step - 1, (), True)
            close_pass()
            with pe.Fori(1, PASSES - 1) as q:
                pe.wait_ge(pass_copied, q)
                open_pass()
                with pe.Fori(0, PASS) as turn:
                    steps(q * PASS + turn + 1, True, turn)
                close_pass()
            pe.wait_ge(pass_copied, PASSES - 1)
            open_pass()
            with pe.Fori(0, PASS) as turn:
                steps(turn + ((PASSES - 1) * PASS + 1), False, turn)
            close_pass()
            pe.wait_ge(pass_copied, PASSES)
            for step in range(PASSES * PASS + 1, STEPS):
                steps(step, False, None, FOLDS[step])

            pe.wait_ge(same_ready, STEPS * GROUPS + E)
            def map_chunk(c, s, n):
                pe.wait_ge(agg_ready, c + 1)
                if not (isinstance(c, int) and c < 2):
                    pe.wait_ge(agg_t_ready, c - 1)
                for t in range(n):
                    last = nc.tensor.transpose(p_prep[s % 2][:, t * P:(t + 1) * P], part[0][:, s, t, :], ident[:, :])
                last.then_inc(agg_t_done, 1)
                pe.wait_ge(agg_t_ready, c + 1)
                if not (isinstance(c, int) and c < 2):
                    pe.wait_ge(z_ready, c - 1)
                for t in range(n):
                    last = nc.tensor.matmul(p_src[s % 2][:, t * D:(t + 1) * D],
                                            lhsT=agg_t[:, s % 2, t * P:(t + 1) * P], rhs=wab[:, 1, :],
                                            start=True, stop=True)
                last.then_inc(map_done, 1)

            for c in range(SLOTS):
                map_chunk(c, c, tiles_of(c))
            with pe.Fori(1, TURNS) as turn:
                for s in range(SLOTS):
                    map_chunk(turn * SLOTS + s, s, QT)
            map_chunk(CHUNKS - 1, 0, 1)


_INS = ['x', 'src', 'edge_attr_128', 'L0_gnn_W1', 'L0_gnn_b1', 'L0_gnn_W2', 'L0_gnn_b2']


def kernel(**inputs):
    import numpy as _np
    import concourse.bacc as _bacc
    from concourse import mybir as _mybir
    from concourse.bass_utils import run_bass_kernel_spmd as _run

    nc = _bacc.Bacc("TRN2", target_bir_lowering=False, num_devices=1)
    arrays, args = {}, []
    for name in _INS:
        a = _np.ascontiguousarray(inputs[name])
        arrays[f"in_{name}_dram"] = a
        args.append(nc.dram_tensor(f"in_{name}_dram", a.shape, _mybir.dt.from_np(a.dtype), kind="ExternalInput").ap())
    args.append(nc.dram_tensor("out_0_dram", inputs["x"].shape, _mybir.dt.float32, kind="ExternalOutput").ap())
    bass_segment_sum_resnorm_kernel(nc, *args)
    r = _run(nc, [arrays], core_ids=[0])
    return r.results[0]["out_0_dram"]
```

```python
import concourse.bass as bass
from concourse import mybir
from contextlib import ExitStack


def bass_segment_sum_resnorm_kernel(nc, x, src, edge_attr, w1, b1, w2, b2, out):
    f32, i32, bf16 = mybir.dt.float32, mybir.dt.int32, mybir.dt.bfloat16
    ALU = mybir.AluOpType
    ACT = mybir.ActivationFunctionType

    P = 128
    NODES, D = x.shape
    EDGES = edge_attr.shape[0]
    HID = w1.shape[1]
    EPS = 1e-5
    DMA = 16

    GT = 3
    GROUPS = 8
    U = GT * GROUPS
    LOADS = 4
    LT = U // LOADS
    BLOCKS = EDGES // (P * U)
    COLS = BLOCKS * U
    STEPS = BLOCKS - 4
    DIRECT_AT = STEPS * U
    DIRECT = COLS - DIRECT_AT
    DU = GROUPS
    ON_DVE = list(range(1, DU, 2))
    ON_ACT = [i for i in range(DU) if i not in ON_DVE]
    PASS = DIRECT // DU
    PASSES = 5
    REST = EDGES - P * COLS
    RT = -(-REST // P)
    LAST = REST - P * (RT - 1)
    REST_GROUPS = [(0, GT), (GT, RT)]
    E = len(REST_GROUPS)
    assert GT < RT <= 2 * GT and DIRECT % DU == 0

    TABLES = 4
    REST_TABLES = [0, 0, 0, 1]
    FIRST_TABLES = [0, 1, 0, 1] + [(2, 0, 1)[u % 3] for u in range(U - 5)] + [3]
    LOOP_TABLES = [u % TABLES for u in range(U)]
    END_TABLES = [u % (TABLES - 1) for u in range(U)]
    ROWS = NODES + P
    SPLIT = 64
    assert ROWS <= SPLIT * 256 and U % (2 * LOADS) == 0 and len(REST_TABLES) == RT

    DW = D + 1
    NT = NODES // P
    NREST = NODES - P * NT
    QT = 4
    SLOTS = 6
    assert NT % QT == 0 and SLOTS % 2 == 0 and NT == (PASSES - 1) * PASS and PASSES * PASS == STEPS - 3
    assert BLOCKS % 8 == 3 and D == P and HID == 2 * P

    CHUNKS = NT // QT + 1
    SHARE = -(-NT // PASSES) * P
    LAST_SHARE = (NT + 1) * P - (PASSES - 1) * SHARE
    SHARE_TILES = SHARE // P
    FOLDS = -(-SHARE // 512)
    assert FOLDS == -(-LAST_SHARE // 512) == 3
    part_loads = DMA * (TABLES - 1)
    ADD_ON_PE = list(range(3, CHUNKS, 2))
    ADD_ON_DVE = [c for c in range(CHUNKS) if c not in ADD_ON_PE]

    def tiles_of(c):
        return 1 if c == CHUNKS - 1 else QT

    def fold_columns(share):
        return [(c, min(c + 512, share)) for c in range(0, share, 512)]

    before = [(REST_TABLES + FIRST_TABLES).count(r) for r in range(TABLES)]
    in_step = [LOOP_TABLES.count(r) for r in range(TABLES)]
    before_end = [before[r] + (STEPS - 2) * in_step[r] for r in range(TABLES)]
    table_total = [before_end[r] + END_TABLES.count(r) for r in range(TABLES)]

    edges_v = edge_attr[0:P * COLS, :].rearrange("(p c) f -> p c f", p=P)
    src_v = src[0:P * COLS].rearrange("(p c) -> p c", p=P)
    x_v = x[0:P * NT, :].rearrange("(p n) f -> p n f", p=P)
    out_v = out[0:P * NT, :].rearrange("(p n) f -> p n f", p=P)
    tables = [nc.dram_tensor(f"table{r}", (ROWS, D), f32, kind="Internal").ap() for r in range(TABLES)]
    tables_v = [t[0:P * NT, :].rearrange("(p n) f -> p n f", p=P) for t in tables]
    ZP = 6
    ZW = ROWS // ZP
    assert ROWS % ZP == 0 and ZP % 2 == 0 and (ROWS * D) // P == ROWS

    with ExitStack() as ctx:
        ctx.enter_context(nc.allow_non_contiguous_dma(reason="b1 as a column, src pieces"))

        def sb(name, shape, dt):
            return ctx.enter_context(nc.sbuf_tensor(name, shape, dt))

        def pb(name):
            return ctx.enter_context(nc.psum_tensor(name, [P, 512], f32))

        def sem(name):
            return ctx.enter_context(nc.semaphore(name))

        src_f = sb("src_f", [P, U + COLS], f32)
        hilo_t = sb("hilo_t", [2 * U, BLOCKS + 1, P], bf16)
        pick_1 = sb("pick_1", [2 * U, U], bf16)
        pick = sb("pick", [2 * U, U, P], bf16)
        data = sb("data", [P, U, DW], f32)
        data_rest = sb("data_rest", [P, RT, DW], f32)
        same = sb("same", [P, 2, GT, P], f32)
        sums = sb("sums", [P, GROUPS + E, GT, DW], f32)
        flag = sb("flag", [P, 2, GT], f32)
        index = sb("index", [P, U + E * GT], i32)
        spare_i = sb("spare_i", [P, 1], i32)
        spare_f = sb("spare_f", [P, 1], f32)
        weight_i = sb("weight_i", [P, 1], i32)
        limit_i = sb("limit_i", [P, 1], i32)
        ident = sb("ident", [P, P], f32)
        ident_b = sb("ident_b", [P, P], bf16)
        w1_sb = sb("w1_sb", [P, 2, HID], f32)
        w2_sb = sb("w2_sb", [P, 2, D], f32)
        b1_sb = sb("b1_sb", [P, 2], f32)
        b2_sb = sb("b2_sb", [1, D], f32)
        w1_t = sb("w1_t", [P, 4, P], f32)
        wab = sb("wab", [P, 2, D], f32)
        bias = sb("bias", [1, D], f32)
        ones = sb("ones", [1, P], f32)
        ones_col = sb("ones_col", [P, 1], f32)
        x_tile = sb("x_tile", [P, D], f32)
        x_rest = sb("x_rest", [P, D], f32)
        x_t = sb("x_t", [P, P], f32)
        y0 = sb("y0", [P, NT + 1, D], f32)
        PW = SLOTS * QT * D
        DIRECT_W = DIRECT * 3 * D // 2
        late = sb("late", [P, max(DIRECT_W, (NT + 1) * D + TABLES * PW)], f32)
        direct = late[:, 0:DIRECT_W].bitcast(bf16).rearrange("p (t h f) -> p t h f", h=3, f=D)
        WH = (BLOCKS + 1) * U
        widths = [WH, WH, WH, ZW]
        starts = [DIRECT_W - sum(widths[i:]) for i in range(len(widths) + 1)]
        assert starts[0] > DIRECT_W // 2
        hilo, src_hi, src_i, zeros = (late[:, a:b] for a, b in zip(starts, starts[1:]))
        hilo = hilo.bitcast(bf16).rearrange("p (b h u) -> p b h u", h=2, u=U)
        src_hi = src_hi.bitcast(i32)
        src_i = src_i.bitcast(i32)
        early = late[:, 0:(NT + 1) * D].rearrange("p (n f) -> p n f", f=D)
        part = [late[:, (NT + 1) * D + r * PW:(NT + 1) * D + (r + 1) * PW].rearrange(
            "p (s n f) -> p s n f", s=SLOTS, f=D) for r in range(TABLES - 1)]
        z = late[:, (NT + 1) * D + (TABLES - 1) * PW:(NT + 1) * D + TABLES * PW].rearrange(
            "p (s n f) -> p s n f", s=SLOTS, f=D)
        agg_t = sb("agg_t", [P, 2, QT * P], f32)
        direct_raw = sb("direct_raw", [P, DU, D], f32)
        share_t = sb("share_t", [P, SHARE], f32)
        share_src = sb("share_src", [P, DIRECT], f32)
        node_f = sb("node_f", [P, SHARE], f32)
        node_last = sb("node_last", [P, P], i32)
        distance = sb("distance", [P, 2, SHARE], bf16)
        node_i = distance[:, :, :].rearrange("p a b -> p (a b)").bitcast(i32)
        onehot = sb("onehot", [P, 3, SHARE], bf16)
        zeros_b = sb("zeros_b", [P, 512], bf16)
        stats = sb("stats", [P, QT, 6], f32)
        mv = sb("mv", [P, SLOTS, QT, 2], f32)
        std = sb("std", [P, SLOTS, QT], f32)
        rstd = sb("rstd", [P, SLOTS, QT], f32)
        shift = sb("shift", [P, SLOTS, QT], f32)
        eps = sb("eps", [P, 1], f32)

        p_src = [pb("p_src0"), pb("p_src1")]
        p_sum = [pb("p_sum0"), pb("p_sum1")]
        p_prep = [pb("p_prep0"), pb("p_prep1")]
        p_xt = pb("p_xt")
        p_y = pb("p_y")
        p_direct = [p_prep[0], p_prep[1], p_xt]
        weight = weight_i[:, :].bitcast(f32)
        limit = limit_i[:, :].bitcast(f32)

        src_loaded = sem("src_loaded")
        rest_loaded = sem("rest_loaded")
        weights_loaded = sem("weights_loaded")
        x_rest_loaded = sem("x_rest_loaded")
        x_loaded = sem("x_loaded")
        data_loaded = [sem(f"data_loaded{q}") for q in range(LOADS)]
        table_zeroed = [[sem(f"table_zeroed{r}_{i}") for i in range(2)] for r in range(TABLES)]
        zeros_ready = sem("zeros_ready")
        fills_ready = sem("fills_ready")
        consts_ready = sem("consts_ready")
        ident_ready = sem("ident_ready")
        data_rest_loaded = sem("data_rest_loaded")
        pool_fills = sem("pool_fills")
        pool_step = sem("pool_step")
        pick_ready = sem("pick_ready")
        dve_step = sem("dve_step")
        hilo_ready = sem("hilo_ready")
        weights_ready = sem("weights_ready")
        prep_done = sem("prep_done")
        prep_copied = sem("prep_copied")
        src_spread = sem("src_spread")
        same_ready = sem("same_ready")
        summed = sem("summed")
        sums_ready = sem("sums_ready")
        flag_ready = sem("flag_ready")
        index_ready = sem("index_ready")
        landed = [sem(f"landed{r}") for r in range(TABLES)]
        w1_t_done = sem("w1_t_done")
        w1_t_ready = sem("w1_t_ready")
        wab_done = sem("wab_done")
        wab_ready = sem("wab_ready")
        x_t_done = sem("x_t_done")
        x_t_ready = sem("x_t_ready")
        y_done = sem("y_done")
        y0_ready = sem("y0_ready")
        raw_loaded = sem("raw_loaded")
        split_step = sem("split_step")
        share_ready = sem("share_ready")
        node_ready = sem("node_ready")
        zeros_b_ready = sem("zeros_b_ready")
        distance_ready = sem("distance_ready")
        onehot_ready = sem("onehot_ready")
        dve_onehot_ready = sem("dve_onehot_ready")
        direct_done = sem("direct_done")
        pass_done = sem("pass_done")
        pass_copied = sem("pass_copied")
        fold_done = sem("fold_done")
        fold_added = sem("fold_added")
        part_loaded = [sem(f"part_loaded{s}") for s in range(SLOTS)]
        early_loaded = sem("early_loaded")
        two_added = sem("two_added")
        half_added = sem("half_added")
        agg_ready = sem("agg_ready")
        agg_t_done = sem("agg_t_done")
        agg_t_ready = sem("agg_t_ready")
        map_done = sem("map_done")
        z_ready = sem("z_ready")
        stats_ready = sem("stats_ready")
        rstd_ready = sem("rstd_ready")
        moments_ready = sem("moments_ready")
        std_ready = sem("std_ready")
        scale_ready = sem("scale_ready")
        result_ready = sem("result_ready")
        stored = sem("stored")

        block = ctx.enter_context(nc.Block())

        @block.sync
        def _(sp):
            sp.dma_start(src_i[:, U:U + COLS], src_v).then_inc(src_loaded, DMA)
            sp.wait_ge(pool_fills, 1)
            sp.dma_start(src_i[:, 0:RT - 1],
                         src[P * COLS:EDGES - LAST].rearrange("(p c) -> p c", p=P)).then_inc(rest_loaded, DMA)
            sp.dma_start(src_i[0:LAST, RT - 1:RT],
                         src[EDGES - LAST:EDGES].rearrange("(p c) -> p c", p=LAST)).then_inc(rest_loaded, DMA)
            sp.wait_ge(fills_ready, 1)
            sp.dma_start(data_rest[:, 0:RT - 1, 0:D],
                         edge_attr[P * COLS:EDGES - LAST, :].rearrange("(p c) f -> p c f", p=P)
                         ).then_inc(data_rest_loaded, DMA)
            sp.dma_start(data_rest[0:LAST, RT - 1, 0:D],
                         edge_attr[EDGES - LAST:EDGES, :]).then_inc(data_rest_loaded, DMA)
            sp.wait_ge(zeros_ready, 1)

            def zero(r, piece):
                if piece >= 2:
                    sp.wait_ge(table_zeroed[r][piece % 2], DMA * (piece // 2))
                sp.dma_start(tables[r].rearrange("a f -> (a f)").rearrange("(p b c) -> p b c", p=P, b=ZP)[:, piece, :],
                             zeros[:, :]).then_inc(table_zeroed[r][piece % 2], DMA)

            def first_load(q):
                sp.dma_start(data[:, q * LT:(q + 1) * LT, 0:D],
                             edges_v[:, q * LT:(q + 1) * LT, :]).then_inc(data_loaded[q], DMA)

            for piece in range(ZP):
                zero(0, piece)
            first_load(0)
            for piece in range(ZP):
                zero(1, piece)
                if piece % 2 and piece // 2 + 1 < LOADS:
                    first_load(piece // 2 + 1)
            sp.dma_start(w1_sb[:, :, :], w1.rearrange("(k p) h -> p k h", p=P)).then_inc(weights_loaded, DMA)
            sp.dma_start(w2_sb[:, :, :], w2.rearrange("(k p) h -> p k h", p=P)).then_inc(weights_loaded, DMA)
            sp.dma_start(b1_sb[:, :], b1.rearrange("(k p) -> p k", p=P)).then_inc(weights_loaded, DMA)
            sp.dma_start(b2_sb[:, :], b2.rearrange("(o f) -> o f", o=1)).then_inc(weights_loaded, DMA)
            sp.dma_start(x_rest[0:NREST, :], x[P * NT:NODES, :]).then_inc(x_rest_loaded, DMA)
            sp.dma_start(x_tile[:, :], x_v[:, 0, :]).then_inc(x_loaded, DMA)
            for r in range(2, TABLES):
                for piece in range(ZP):
                    zero(r, piece)

            def load_edges(step):
                for q in range(LOADS):
                    sp.wait_ge(summed, step * GROUPS + (E + (q + 1) * GROUPS // LOADS))
                    sp.dma_start(data[:, q * LT:(q + 1) * LT, 0:D],
                                 edges_v[:, bass.ds(step * U + (U + q * LT), LT), :]
                                 ).then_inc(data_loaded[q], DMA)

            def load_x(step):
                sp.wait_ge(y0_ready, step + 1)
                sp.dma_start(x_tile[:, :], x_v[:, bass.ds(step, 1), :].rearrange("p n f -> p (n f)")
                             ).then_inc(x_loaded, DMA)

            sp.dma_start(direct_raw[:, :, :], edges_v[:, DIRECT_AT:DIRECT_AT + DU, :]).then_inc(raw_loaded, DMA)
            load_edges(0)
            with sp.Fori(1, PASS) as step:
                sp.wait_ge(split_step, step * 4)
                sp.dma_start(direct_raw[:, :, :], edges_v[:, bass.ds(step * DU + DIRECT_AT, DU), :]
                             ).then_inc(raw_loaded, DMA)
                load_edges(step)
                load_x(step)
            with sp.Fori(PASS, NT) as step:
                load_edges(step)
                load_x(step)
            with sp.Fori(NT, STEPS - 1) as step:
                load_edges(step)

            out_of_use = TABLES - 1
            sp.wait_ge(direct_done, PASSES * DIRECT)
            sp.wait_ge(landed[out_of_use], DMA * table_total[out_of_use])
            sp.dma_start(early[:, NT, :], tables[out_of_use][P * NT:P * NT + P, :]).then_inc(early_loaded, DMA)
            for q in range(NT // QT):
                sp.wait_ge(landed[0], DMA * (before_end[0] + q // 2))
                sp.dma_start(early[:, q * QT:(q + 1) * QT, :], tables_v[out_of_use][:, q * QT:(q + 1) * QT, :]
                             ).then_inc(early_loaded, DMA)

            for r in range(TABLES - 1):
                sp.wait_ge(landed[r], DMA * table_total[r])
            def load_chunk(c, s):
                for r in range(TABLES - 1):
                    sp.dma_start(part[r][:, s, :, :], tables_v[r][:, bass.ds(c * QT, QT), :]
                                 ).then_inc(part_loaded[s], DMA)

            for c in range(CHUNKS - 1):
                if c >= SLOTS:
                    sp.wait_ge(agg_t_done, c - (SLOTS - 1))
                load_chunk(c, c % SLOTS)
            sp.wait_ge(agg_t_done, CHUNKS - SLOTS)
            for r in range(TABLES - 1):
                sp.dma_start(part[r][:, 0, 0, :], tables[r][P * NT:P * NT + P, :]).then_inc(part_loaded[0], DMA)

        @block.gpsimd
        def _(pool):
            nc.gpsimd.iota(src_i[:, RT - 1:U], [[0, U - RT + 1]], base=NODES, channel_multiplier=1
                           ).then_inc(pool_fills, 1)
            nc.gpsimd.memset(ident_b[:, :], 0.0)
            nc.gpsimd.memset(pick_1[:, :], 0.0)
            nc.gpsimd.memset(ident[:, :], 0.0).then_inc(pool_step, 1)
            pool.wait_ge(pool_step, 1)
            nc.gpsimd.affine_select(out=pick_1[:, :], in_=pick_1[:, :], compare_op=ALU.not_equal, fill=1.0,
                                    base=0, pattern=[[-1, U]], channel_multiplier=1).then_inc(pool_step, 1)
            pool.wait_ge(pool_step, 2)
            nc.gpsimd.affine_select(out=pick_1[:, :], in_=pick_1[:, :], compare_op=ALU.not_equal, fill=1.0,
                                    base=-U, pattern=[[-1, U]], channel_multiplier=1).then_inc(pool_step, 1)
            nc.gpsimd.affine_select(out=ident_b[:, :], in_=ident_b[:, :], compare_op=ALU.not_equal, fill=1.0,
                                    base=0, pattern=[[-1, P]], channel_multiplier=1)
            nc.gpsimd.iota(spare_i[:, :], [[0, 1]], base=NODES, channel_multiplier=1)
            nc.gpsimd.iota(weight_i[:, :], [[0, 1]], base=(127 + 60) << 23, channel_multiplier=-(1 << 23))
            nc.gpsimd.iota(limit_i[:, :], [[0, 1]], base=((127 + 61) << 23) + (1 << 21),
                           channel_multiplier=-(1 << 23)).then_inc(consts_ready, 1)
            nc.gpsimd.affine_select(out=ident[:, :], in_=ident[:, :], compare_op=ALU.not_equal, fill=1.0,
                                    base=0, pattern=[[-1, P]], channel_multiplier=1).then_inc(ident_ready, 1)
            nc.gpsimd.iota(node_last[:, :], [[1, P]], base=P * NT - (PASSES - 1) * SHARE_TILES, channel_multiplier=0)
            nc.gpsimd.iota(node_i[:, :], [[1, SHARE_TILES], [NT, P]], base=0, channel_multiplier=0
                           ).then_inc(node_ready, 1)

            def scatter(slot, r, done, group_count):
                for i in range(2):
                    pool.wait_ge(table_zeroed[r][i], DMA * ZP // 2)
                if group_count is not None:
                    pool.wait_ge(index_ready, group_count)
                if not (isinstance(done, int) and done == 0):
                    pool.wait_ge(landed[r], done)
                pool.indirect_dma_start(
                    out=tables[r][:, :], out_offset=bass.IndirectOffsetOnAxis(ap=index[:, slot:slot + 1], axis=0),
                    in_=sums[:, slot // GT, slot % GT, 0:D], in_offset=None,
                    compute_op=ALU.add).then_inc(landed[r], DMA)

            for t, r in enumerate(REST_TABLES):
                scatter(U + t, r, DMA * REST_TABLES[:t].count(r), t // GT + 1 if t % GT == 0 else None)
            for u, r in enumerate(FIRST_TABLES):
                scatter(u, r, DMA * (REST_TABLES + FIRST_TABLES[:u]).count(r),
                        E + u // GT + 1 if u % GT == 0 else None)

            landed_count = [pool.alloc_register(f"landed_count{r}") for r in range(TABLES)]
            index_count = pool.alloc_register("index_count")
            for r in range(TABLES):
                pool.reg_mov(landed_count[r], DMA * (before[r] - 1))
            pool.reg_mov(index_count, E + GROUPS)
            assert all(n > 0 for n in before)
            with pool.Fori(1, STEPS - 1) as step:
                for u, r in enumerate(LOOP_TABLES):
                    pool.reg_add(landed_count[r], landed_count[r], DMA)
                    if u % GT == 0:
                        pool.reg_add(index_count, index_count, 1)
                    scatter(u, r, landed_count[r], index_count if u % GT == 0 else None)
            for u, r in enumerate(END_TABLES):
                scatter(u, r, DMA * (before_end[r] + END_TABLES[:u].count(r)),
                        E + (STEPS - 1) * GROUPS + u // GT + 1 if u % GT == 0 else None)

            pool.wait_ge(early_loaded, DMA * CHUNKS)
            for c in range(CHUNKS):
                s, n = c % SLOTS, tiles_of(c)
                pool.wait_ge(part_loaded[s], part_loads * (c // SLOTS + 1))
                nc.gpsimd.tensor_tensor(out=part[1][:, s, 0:n, :], in0=part[1][:, s, 0:n, :],
                                        in1=part[2][:, s, 0:n, :], op=ALU.add).then_inc(two_added, 1)
                pool.wait_ge(two_added, c + 1)
                nc.gpsimd.tensor_tensor(out=part[1][:, s, 0:n, :], in0=part[1][:, s, 0:n, :],
                                        in1=early[:, c * QT:c * QT + n, :], op=ALU.add).then_inc(half_added, 1)

        @block.scalar
        def _(act):
            act.wait_ge(fills_ready, 2)
            nc.scalar.activation(std[:, 0, 0:1], eps[:, :], ACT.Sqrt)
            act.wait_ge(pool_step, 3)
            nc.scalar.copy(pick[:, :, :], pick_1[:, :].unsqueeze(2).to_broadcast([2 * U, U, P])).then_inc(pick_ready, 1)

            def copy_prep(first, i, count):
                act.wait_ge(prep_done, count)
                nc.scalar.copy(hilo_t[:, bass.ds(first, 4), :],
                               p_prep[i][0:2 * U, :].rearrange("p (b c) -> p b c", c=P)).then_inc(prep_copied, 1)

            copy_prep(0, 0, 1)

            def take_sums(slot, bank, tiles, count):
                act.wait_ge(summed, count)
                nc.scalar.copy(sums[:, slot, 0:tiles, :], p_sum[bank][:, 0:tiles * DW].rearrange(
                    "p (t c) -> p t c", c=DW)).then_inc(sums_ready, 1)

            for e, (t0, t1) in enumerate(REST_GROUPS):
                take_sums(GROUPS + e, e, t1 - t0, e + 1)
            for k in range(GROUPS):
                take_sums(k, k % 2, GT, E + k + 1)

            with act.Fori(0, BLOCKS // 8) as turn:
                for i in range(2):
                    copy_prep(turn * 8 + (4 + 4 * i), 1 - i, turn * 2 + (i + 2))

            act.wait_ge(w1_t_done, 1)
            nc.scalar.copy(w1_t[:, :, :], p_xt[:, :].rearrange("p (b c) -> p b c", c=P)).then_inc(w1_t_ready, 1)
            act.wait_ge(wab_done, 1)
            nc.scalar.copy(wab[:, :, :], p_y[:, 0:2 * D].rearrange("p (b c) -> p b c", c=D))
            nc.scalar.copy(bias[:, :], p_y[0:1, 2 * D:3 * D]).then_inc(wab_ready, 1)

            def copy_x_t(n):
                act.wait_ge(x_t_done, n + 1)
                if not (isinstance(n, int) and n == 0):
                    act.wait_ge(y_done, n)
                nc.scalar.copy(x_t[:, :], p_y[:, D:D + P]).then_inc(x_t_ready, 1)

            copy_x_t(0)

            def select(step, tile, j, width):
                count = (step - 1) * len(ON_ACT) + j
                nc.scalar.activation(distance[:, j % 2, 0:width], node_f[:, 0:width], ACT.Abs,
                                     bias=share_src[:, bass.ds(tile, 1)], scale=-1.0).then_inc(distance_ready, 1)
                act.wait_ge(distance_ready, count + 1)
                if not (isinstance(count, int) and count < 2):
                    before_it = ON_ACT[j - 2] if j >= 2 else ON_ACT[j - 2] - DU
                    act.wait_ge(direct_done, (step - 1) * DU + (before_it + 1))
                nc.scalar.activation(onehot[:, j % 2, 0:width], distance[:, j % 2, 0:width], ACT.Relu,
                                     bias=ones_col[:, :], scale=-1.0).then_inc(onehot_ready, 1)

            def copy_pass(q, share):
                act.wait_ge(pass_done, q + 1)
                for (c0, c1), bank in zip(fold_columns(share), p_direct):
                    last = nc.scalar.copy(share_t[:, c0:c1], bank[:, 0:c1 - c0])
                last.then_inc(pass_copied, 1)

            def steps(step, slot_landed, x_at, turn=None, width=SHARE):
                for k in range(GROUPS):
                    if turn is not None and k in ON_ACT:
                        select(step, turn * DU + k, ON_ACT.index(k), width)
                    for u in range(k * GT, (k + 1) * GT):
                        act.wait_ge(*slot_landed(u))
                    take_sums(k, k % 2, GT, step * GROUPS + (E + k + 1))
                    if x_at is not None and k == x_at + 1:
                        copy_x_t(step)

            def after_first(u):
                r = FIRST_TABLES[u]
                return landed[r], DMA * (REST_TABLES + FIRST_TABLES[:u + 1]).count(r)

            def after(step):
                def slot_landed(u):
                    r = LOOP_TABLES[u]
                    return landed[r], (step - 2) * (DMA * in_step[r]) + DMA * (
                        before[r] + LOOP_TABLES[:u + 1].count(r))
                return slot_landed

            act.wait_ge(share_ready, 1)
            steps(1, after_first, 0, 0)
            with act.Fori(2, PASS + 1) as step:
                steps(step, after(step), 0, step - 1)
            copy_pass(0, SHARE)
            with act.Fori(1, PASSES - 1) as q:
                act.wait_ge(share_ready, q + 1)
                steps(q * PASS + 1, after(q * PASS + 1), FOLDS + 1, 0)
                with act.Fori(1, PASS) as turn:
                    step = q * PASS + turn + 1
                    steps(step, after(step), 0, turn)
                copy_pass(q, SHARE)
            act.wait_ge(share_ready, PASSES + 1)
            with act.Fori(0, PASS) as turn:
                step = turn + ((PASSES - 1) * PASS + 1)
                steps(step, after(step), None, turn, LAST_SHARE)
            copy_pass(PASSES - 1, LAST_SHARE)
            for step in range(PASSES * PASS + 1, STEPS):
                steps(step, after(step), None)

            def copy_agg_t(s, n, count):
                act.wait_ge(agg_t_done, count + 1)
                if count >= 2:
                    act.wait_ge(map_done, count - 1)
                nc.scalar.copy(agg_t[:, s % 2, 0:n * P], p_prep[s % 2][:, 0:n * P]).then_inc(agg_t_ready, 1)

            def root(s, n, count):
                act.wait_ge(moments_ready, count + 1)
                nc.scalar.activation(std[:, s, 0:n], mv[:, s, 0:n, 1], ACT.Sqrt, bias=eps[:, :]
                                     ).then_inc(std_ready, 1)

            def normalise(c, s, n, tile):
                act.wait_ge(scale_ready, c + 1)
                for t in range(n):
                    last = nc.scalar.activation(y0[:, bass.ds(tile + t, 1), :].rearrange("p n f -> p (n f)"),
                                                z[:, s, t, :], ACT.Identity,
                                                bias=shift[:, s, t:t + 1], scale=rstd[:, s, t:t + 1])
                last.then_inc(result_ready, 1)

            def store_chunk(c):
                act.wait_ge(result_ready, c + 1)
                act.dma_start(out_v[:, bass.ds(c * QT, QT), :], y0[:, bass.ds(c * QT, QT), :]
                              ).then_inc(stored, DMA)

            for c in range(CHUNKS + 3):
                if c < CHUNKS:
                    copy_agg_t(c % SLOTS, tiles_of(c), c)
                if 2 <= c < CHUNKS + 2:
                    root((c - 2) % SLOTS, tiles_of(c - 2), c - 2)
                if c >= 3:
                    normalise(c - 3, (c - 3) % SLOTS, tiles_of(c - 3), (c - 3) * QT)
                if c >= 4:
                    store_chunk(c - 4)
            act.wait_ge(result_ready, CHUNKS)
            act.dma_start(out[P * NT:NODES, :], y0[0:NREST, NT, :]).then_inc(stored, DMA)
            act.wait_ge(stored, DMA * CHUNKS)

        @block.vector
        def _(dve):
            nc.vector.memset(zeros[:, :], 0.0).then_inc(zeros_ready, 1)
            nc.vector.memset(data_rest[:, RT - 1, :], 0.0)
            nc.vector.memset(x_rest[:, :], 0.0).then_inc(fills_ready, 1)
            nc.vector.memset(ones[:, :], 1.0)
            nc.vector.memset(ones_col[:, :], 1.0)
            nc.vector.memset(zeros_b[:, :], 0.0).then_inc(zeros_b_ready, 1)
            nc.vector.memset(eps[:, :], EPS).then_inc(fills_ready, 1)
            dve.wait_ge(src_loaded, DMA)
            dve.wait_ge(rest_loaded, 2 * DMA)
            for i, (b0, b1_) in enumerate(((0, 4), (4, BLOCKS + 1))):
                c0, c1 = b0 * U, b1_ * U
                hi = src_hi[:, c0:c1]
                nc.vector.tensor_scalar(hi, src_i[:, c0:c1], -SPLIT, None, ALU.bitwise_and).then_inc(dve_step, 1)
                nc.vector.tensor_copy(src_f[:, c0:c1], src_i[:, c0:c1])
                dve.wait_ge(dve_step, i + 1)
                hi = hi.rearrange("p (b w) -> p b w", w=U)
                nc.vector.tensor_copy(hilo[:, b0:b1_, 0, :], hi)
                nc.vector.tensor_tensor(hilo[:, b0:b1_, 1, :], src_i[:, c0:c1].rearrange("p (b w) -> p b w", w=U),
                                        hi, ALU.subtract).then_inc(hilo_ready, 1)
                if i == 0:
                    dve.wait_ge(consts_ready, 1)
                    nc.vector.tensor_copy(spare_f[:, :], spare_i[:, :])
                    nc.vector.tensor_copy(data_rest[:, :, D:DW], weight.unsqueeze(1).to_broadcast([P, RT, 1]))
                    nc.vector.tensor_copy(data[:, :, D:DW], weight.unsqueeze(1).to_broadcast([P, U, 1])
                                          ).then_inc(weights_ready, 1)
            dve.wait_ge(weights_ready, 1)
            dve.wait_ge(hilo_ready, 2)
            dve.wait_ge(node_ready, 1)
            nc.vector.tensor_copy(node_f[:, :], node_i[:, :])
            nc.vector.tensor_copy(share_src[:, :], src_f[:, U + DIRECT_AT:U + COLS]).then_inc(share_ready, 1)

            def compare(k, tiles, col, group):
                dve.wait_ge(src_spread, group + 1)
                if not (isinstance(group, int) and group < 2):
                    dve.wait_ge(summed, group - 1)
                nc.vector.tensor_tensor(
                    same[:, k % 2, 0:tiles, :], p_src[k % 2][:, 0:tiles * P].rearrange("p (t c) -> p t c", c=P),
                    src_f[:, bass.ds(col, tiles)].unsqueeze(2).to_broadcast([P, tiles, P]), ALU.is_equal
                ).then_inc(same_ready, 1)

            def rows(k, tiles, col, group):
                dve.wait_ge(sums_ready, group + 1)
                nc.vector.tensor_scalar(flag[:, k % 2, 0:tiles], sums[:, k, 0:tiles, D], limit, spare_f[:, :],
                                        ALU.is_gt, ALU.mult).then_inc(flag_ready, 1)
                dve.wait_ge(flag_ready, group + 1)
                nc.vector.tensor_tensor(index[:, k * GT:k * GT + tiles], flag[:, k % 2, 0:tiles],
                                        src_f[:, bass.ds(col, tiles)], ALU.max).then_inc(index_ready, 1)

            def add_y0(n, tile, x_used):
                dve.wait_ge(y_done, n + 1)
                nc.vector.tensor_tensor(y0[:, bass.ds(tile, 1), :].rearrange("p n f -> p (n f)"),
                                        p_y[:, 0:D], x_used[:, :], ALU.add).then_inc(y0_ready, 1)

            for e, (t0, t1) in enumerate(REST_GROUPS):
                compare(GROUPS + e, t1 - t0, t0, e)
                if e:
                    rows(GROUPS + e - 1, GT, 0, e - 1)
            rows(GROUPS + E - 1, RT - GT, GT, E - 1)

            def split(i, step):
                if i == 0:
                    dve.wait_ge(raw_loaded, step * DMA)
                else:
                    dve.wait_ge(split_step, step * 4 - (4 - i))
                part_of = direct[:, bass.ds(step * DU - DU, DU), (0, 0, 1, 2)[i], :]
                if i % 2 == 0:
                    nc.vector.tensor_scalar(part_of, direct_raw[:, :, :], 1.0, None, ALU.mult).then_inc(split_step, 1)
                elif i == 1:
                    nc.vector.tensor_tensor(direct_raw[:, :, :], direct_raw[:, :, :], part_of, ALU.subtract
                                            ).then_inc(split_step, 1)
                else:
                    nc.vector.tensor_tensor(part_of, direct_raw[:, :, :], direct[:, bass.ds(step * DU - DU, DU), 1, :],
                                            ALU.subtract).then_inc(split_step, 1)

            def next_share(q):
                dve.wait_ge(distance_ready, (q + 1) * (PASS * len(ON_ACT)))
                dve.wait_ge(dve_onehot_ready, (q + 1) * (PASS * len(ON_DVE)))
                nc.vector.tensor_scalar(share_src[:, :], share_src[:, :], -float(SHARE_TILES), None, ALU.add
                                        ).then_inc(share_ready, 1)

            def select(step, tile, j, width):
                if not (isinstance(step, int) and step == 1 and j == 0):
                    before_it = ON_DVE[j - 1] if j else ON_DVE[-1] - DU
                    dve.wait_ge(direct_done, (step - 1) * DU + (before_it + 1))
                nc.vector.tensor_tensor(onehot[:, 2, 0:width], node_f[:, 0:width],
                                        share_src[:, bass.ds(tile, 1)].to_broadcast([P, width]), ALU.is_equal
                                        ).then_inc(dve_onehot_ready, 1)

            def add_fold(q, f, tiles):
                dve.wait_ge(fold_done, q * FOLDS + (f + 1))
                folded = y0[:, bass.ds(q * SHARE_TILES + f * QT, tiles), :]
                nc.vector.tensor_tensor(folded, folded, p_y[:, 0:tiles * D].rearrange("p (t c) -> p t c", c=D),
                                        ALU.add).then_inc(fold_added, 1)

            def steps(step, x_at, turn=None, split_next=False, fold=None, width=SHARE):
                for k in range(GROUPS):
                    compare(k, GT, step * U + (U + k * GT), step * GROUPS + (E + k))
                    if fold is not None and 2 <= k < 2 + FOLDS:
                        q, share = fold
                        c0, c1 = fold_columns(share)[k - 2]
                        add_fold(q, k - 2, (c1 - c0) // P)
                    if k:
                        rows(k - 1, GT, step * U + (U + (k - 1) * GT), step * GROUPS + (E + k - 1))
                    if turn is not None and k + 1 in ON_DVE:
                        select(step, turn * DU + (k + 1), ON_DVE.index(k + 1), width)
                    if x_at is not None and k == min(x_at + 5, GROUPS - 1):
                        add_y0(step, step - 1, x_tile)
                    if split_next and k >= GROUPS - 4:
                        split(k - (GROUPS - 4), step + 1)
                rows(GROUPS - 1, GT, step * U + (U + (GROUPS - 1) * GT), step * GROUPS + (E + GROUPS - 1))

            steps(0, None)
            add_y0(0, NT, x_rest)
            for i in range(4):
                split(i, 1)
            dve.wait_ge(share_ready, 1)
            steps(1, 0, 0, True)
            with dve.Fori(2, PASS) as step:
                steps(step, 0, step - 1, True)
            steps(PASS, 0, PASS - 1)
            next_share(0)
            with dve.Fori(1, PASSES - 1) as q:
                dve.wait_ge(share_ready, q + 1)
                steps(q * PASS + 1, FOLDS + 1, 0, False, (q - 1, SHARE))
                with dve.Fori(1, PASS) as turn:
                    steps(q * PASS + turn + 1, 0, turn)
                next_share(q)
            nc.vector.tensor_copy(node_f[:, LAST_SHARE - P:LAST_SHARE], node_last[:, :]).then_inc(share_ready, 1)
            dve.wait_ge(share_ready, PASSES + 1)
            steps((PASSES - 1) * PASS + 1, None, 0, False, (PASSES - 2, SHARE), LAST_SHARE)
            with dve.Fori(1, PASS) as turn:
                steps(turn + ((PASSES - 1) * PASS + 1), None, turn, False, None, LAST_SHARE)
            steps(PASSES * PASS + 1, None, None, False, (PASSES - 1, LAST_SHARE))
            for step in range(PASSES * PASS + 2, STEPS):
                steps(step, None)

            def add_parts(c, s, n, loads):
                dve.wait_ge(part_loaded[s], loads)
                dve.wait_ge(half_added, c + 1)
                nc.vector.tensor_tensor(part[0][:, s, 0:n, :], part[0][:, s, 0:n, :], part[1][:, s, 0:n, :],
                                        ALU.add).then_inc(agg_ready, 1)

            def moments(c, s, n, tile):
                dve.wait_ge(map_done, c + 1)
                if c >= SLOTS:
                    dve.wait_ge(result_ready, c - (SLOTS - 1))
                nc.vector.tensor_tensor(z[:, s, 0:n, :], p_src[s % 2][:, 0:n * D].rearrange(
                    "p (t c) -> p t c", c=D), y0[:, bass.ds(tile, n), :], ALU.add).then_inc(z_ready, 1)
                dve.wait_ge(z_ready, c + 1)
                for t in range(n):
                    last = nc.vector.bn_stats(stats[:, t, :], z[:, s, t, :])
                last.then_inc(stats_ready, 1)

            def aggregate(c, s, n):
                for t in range(n):
                    last = nc.vector.bn_aggr(mv[:, s, t, :], stats[:, t, :])
                last.then_inc(moments_ready, 1)

            def scales(c, s, n):
                dve.wait_ge(std_ready, c + 1)
                dve.wait_ge(stats_ready, min(c + 2, CHUNKS))
                nc.vector.reciprocal(rstd[:, s, 0:n], std[:, s, 0:n]).then_inc(rstd_ready, 1)
                if c + 1 < CHUNKS:
                    aggregate(c + 1, (s + 1) % SLOTS, tiles_of(c + 1))
                dve.wait_ge(rstd_ready, c + 1)
                nc.vector.scalar_tensor_tensor(shift[:, s, 0:n], mv[:, s, 0:n, 0], -1.0, rstd[:, s, 0:n],
                                               ALU.mult, ALU.mult).then_inc(scale_ready, 1)

            for c in range(CHUNKS + 3):
                if c in ADD_ON_DVE:
                    add_parts(c, c % SLOTS, tiles_of(c), part_loads * (c // SLOTS + 1))
                if 2 <= c < CHUNKS + 2:
                    moments(c - 2, (c - 2) % SLOTS, tiles_of(c - 2), (c - 2) * QT)
                if c == 2:
                    dve.wait_ge(stats_ready, 1)
                    aggregate(0, 0, tiles_of(0))
                if c >= 3:
                    scales(c - 3, (c - 3) % SLOTS, tiles_of(c - 3))

        @block.tensor
        def _(pe):
            pe.wait_ge(consts_ready, 1)
            pe.wait_ge(hilo_ready, 1)

            def prepare(first, i):
                for b in range(4):
                    last = nc.tensor.matmul(
                        p_prep[i][0:2 * U, b * P:(b + 1) * P],
                        lhsT=hilo[:, bass.ds(first + b, 1), :, :].rearrange("p b h u -> p (b h u)"),
                        rhs=ident_b[:, :], start=True, stop=True)
                last.then_inc(prep_done, 1)

            prepare(0, 0)
            def turn_x(n, x_used):
                if not (isinstance(n, int) and n == 0):
                    pe.wait_ge(y0_ready, n)
                nc.tensor.transpose(p_y[:, D:D + P], x_used[:, :], ident[:, :]).then_inc(x_t_done, 1)

            def map_x(n):
                pe.wait_ge(x_t_ready, n + 1)
                nc.tensor.matmul(p_y[:, 0:D], lhsT=x_t[:, :], rhs=wab[:, 0, :], start=True, stop=False)
                nc.tensor.matmul(p_y[:, 0:D], lhsT=ones[:, :], rhs=bias[:, :], start=False, stop=True
                                 ).then_inc(y_done, 1)

            pe.wait_ge(prep_copied, 1)
            pe.wait_ge(pick_ready, 1)

            def spread(k, tiles, block_at):
                for t in range(tiles):
                    last = nc.tensor.matmul(
                        p_src[k % 2][:, t * P:(t + 1) * P],
                        lhsT=pick[:, k * GT + t, :],
                        rhs=hilo_t[:, bass.ds(block_at, 1), :].rearrange("q b j -> q (b j)"), start=True, stop=True)
                last.then_inc(src_spread, 1)

            def add_up(k, tiles, rows_of, group):
                pe.wait_ge(same_ready, group + 1)
                if not (isinstance(group, int) and group < 2):
                    pe.wait_ge(sums_ready, group - 1)
                for t in range(tiles):
                    last = nc.tensor.matmul(p_sum[k % 2][:, t * DW:(t + 1) * DW], lhsT=same[:, k % 2, t, :],
                                            rhs=rows_of[:, t, :], start=True, stop=True)
                last.then_inc(summed, 1)

            for e, (t0, t1) in enumerate(REST_GROUPS):
                for t in range(t0, t1):
                    last = nc.tensor.matmul(p_src[e][:, (t - t0) * P:(t - t0 + 1) * P], lhsT=pick[:, t, :],
                                            rhs=hilo_t[:, 0, :], start=True, stop=True)
                last.then_inc(src_spread, 1)
            pe.wait_ge(weights_ready, 1)
            pe.wait_ge(data_rest_loaded, 2 * DMA)
            for e, (t0, t1) in enumerate(REST_GROUPS):
                add_up(e, t1 - t0, data_rest[:, t0:t1, :], e)

            def open_pass(share):
                for (c0, c1), bank in zip(fold_columns(share), p_direct):
                    nc.tensor.matmul(bank[:, 0:c1 - c0], lhsT=zeros_b[:, 0:P], rhs=zeros_b[:, 0:c1 - c0],
                                     start=True, stop=False)

            def close_pass(share):
                for (c0, c1), bank in zip(fold_columns(share), p_direct):
                    last = nc.tensor.matmul(bank[:, 0:c1 - c0], lhsT=zeros_b[:, 0:P], rhs=zeros_b[:, 0:c1 - c0],
                                            start=False, stop=True)
                last.then_inc(pass_done, 1)

            def add_direct(step, tile, i, share):
                if i in ON_DVE:
                    slot = 2
                    pe.wait_ge(dve_onehot_ready, (step - 1) * len(ON_DVE) + (ON_DVE.index(i) + 1))
                else:
                    slot = ON_ACT.index(i) % 2
                    pe.wait_ge(onehot_ready, (step - 1) * len(ON_ACT) + (ON_ACT.index(i) + 1))
                for h in range(3):
                    for (c0, c1), bank in zip(fold_columns(share), p_direct):
                        last = nc.tensor.matmul(
                            bank[:, 0:c1 - c0],
                            lhsT=direct[:, bass.ds(tile, 1), h, :].rearrange("p t f -> p (t f)"),
                            rhs=onehot[:, slot, c0:c1], start=False, stop=False)
                last.then_inc(direct_done, 1)

            def map_fold(q, f, tiles):
                if f or isinstance(q, int):
                    pe.wait_ge(fold_added, q * FOLDS + f)
                for t in range(tiles):
                    last = nc.tensor.matmul(p_y[:, t * D:(t + 1) * D],
                                            lhsT=share_t[:, (f * QT + t) * P:(f * QT + t + 1) * P],
                                            rhs=wab[:, 1, :], start=True, stop=True)
                last.then_inc(fold_done, 1)

            def steps(step, x_at, turn=None, share=SHARE, split_first=False, opens=None, fold=None):
                for k in range(GROUPS):
                    group = step * GROUPS + (E + k)
                    if k == 0:
                        spread(0, GT, step + 1)
                    if k + 1 < GROUPS:
                        spread(k + 1, GT, step + 1)
                    if k % (GROUPS // LOADS) == 0:
                        pe.wait_ge(data_loaded[k // (GROUPS // LOADS)], step * DMA + DMA)
                    add_up(k, GT, data[:, k * GT:(k + 1) * GT, :], group)
                    if x_at is not None and k == x_at:
                        pe.wait_ge(x_loaded, step * DMA)
                        if fold is not None:
                            pe.wait_ge(fold_added, fold[0] * FOLDS + FOLDS)
                        turn_x(step, x_tile)
                    if x_at is not None and k == min(x_at + 3, GROUPS - 2):
                        map_x(step)
                    if k == 0 and opens is not None:
                        pe.wait_ge(pass_copied, opens)
                        open_pass(share)
                    if k == 0 and split_first:
                        pe.wait_ge(split_step, step * 4)
                    if turn is not None:
                        add_direct(step, turn * DU + k, k, share)
                    if fold is not None and 1 <= k < 1 + FOLDS:
                        q, folded = fold
                        if k == 1:
                            pe.wait_ge(pass_copied, q + 1)
                            pe.wait_ge(y0_ready, min(step, NT + 1) if isinstance(step, int) else step)
                        c0, c1 = fold_columns(folded)[k - 1]
                        map_fold(q, k - 1, (c1 - c0) // P)

            steps(0, None)

            pe.wait_ge(hilo_ready, 2)
            with pe.Fori(0, BLOCKS // 8) as turn:
                for i in range(2):
                    pe.wait_ge(prep_copied, turn * 2 + 1)
                    prepare(turn * 8 + (4 + 4 * i), 1 - i)

            pe.wait_ge(weights_loaded, 4 * DMA)
            pe.wait_ge(ident_ready, 1)
            for k in range(2):
                for h in range(2):
                    last = nc.tensor.transpose(p_xt[:, (2 * k + h) * P:(2 * k + h + 1) * P],
                                               w1_sb[:, k, h * P:(h + 1) * P], ident[:, :])
            last.then_inc(w1_t_done, 1)
            pe.wait_ge(w1_t_ready, 1)
            for k in range(2):
                for h in range(2):
                    nc.tensor.matmul(p_y[:, k * D:(k + 1) * D], lhsT=w1_t[:, 2 * k + h, :], rhs=w2_sb[:, h, :],
                                     start=(h == 0), stop=(h == 1))
            for h in range(2):
                nc.tensor.matmul(p_y[0:1, 2 * D:3 * D], lhsT=b1_sb[:, h:h + 1], rhs=w2_sb[:, h, :],
                                 start=(h == 0), stop=False)
            nc.tensor.matmul(p_y[0:1, 2 * D:3 * D], lhsT=ones[0:1, 0:1], rhs=b2_sb[:, :],
                             start=False, stop=True).then_inc(wab_done, 1)

            pe.wait_ge(wab_ready, 1)
            pe.wait_ge(x_rest_loaded, DMA)
            turn_x(0, x_rest)
            map_x(0)
            pe.wait_ge(prep_copied, BLOCKS // 4 + 1)

            pe.wait_ge(zeros_b_ready, 1)
            open_pass(SHARE)
            with pe.Fori(1, PASS + 1) as step:
                steps(step, 0, step - 1, SHARE, True)
            close_pass(SHARE)
            with pe.Fori(1, PASSES - 1) as q:
                steps(q * PASS + 1, FOLDS + 1, 0, SHARE, False, q, (q - 1, SHARE))
                with pe.Fori(1, PASS) as turn:
                    steps(q * PASS + turn + 1, 0, turn)
                close_pass(SHARE)
            steps((PASSES - 1) * PASS + 1, None, 0, LAST_SHARE, False, PASSES - 1, (PASSES - 2, SHARE))
            with pe.Fori(1, PASS) as turn:
                steps(turn + ((PASSES - 1) * PASS + 1), None, turn, LAST_SHARE)
            close_pass(LAST_SHARE)
            steps(PASSES * PASS + 1, None, None, LAST_SHARE, False, None, (PASSES - 1, LAST_SHARE))
            for step in range(PASSES * PASS + 2, STEPS):
                steps(step, None)

            pe.wait_ge(same_ready, STEPS * GROUPS + E)
            def turn_chunk(c, s, n):
                if c in ADD_ON_DVE:
                    pe.wait_ge(agg_ready, ADD_ON_DVE.index(c) + 1)
                else:
                    pe.wait_ge(half_added, c + 1)
                if c >= 2:
                    pe.wait_ge(agg_t_ready, c - 1)
                for t in range(n):
                    turned = p_prep[s % 2][:, t * P:(t + 1) * P]
                    if c in ADD_ON_DVE:
                        last = nc.tensor.transpose(turned, part[0][:, s, t, :], ident[:, :])
                    else:
                        for r in range(2):
                            last = nc.tensor.matmul(turned, lhsT=part[r][:, s, t, :], rhs=ident[:, :],
                                                    start=(r == 0), stop=(r == 1))
                last.then_inc(agg_t_done, 1)

            def map_chunk(c, s, n):
                pe.wait_ge(agg_t_ready, c + 1)
                if c >= 2:
                    pe.wait_ge(z_ready, c - 1)
                for t in range(n):
                    last = nc.tensor.matmul(p_src[s % 2][:, t * D:(t + 1) * D],
                                            lhsT=agg_t[:, s % 2, t * P:(t + 1) * P], rhs=wab[:, 1, :],
                                            start=True, stop=True)
                last.then_inc(map_done, 1)

            for c in range(CHUNKS + 1):
                if c < CHUNKS:
                    turn_chunk(c, c % SLOTS, tiles_of(c))
                if c >= 1:
                    map_chunk(c - 1, (c - 1) % SLOTS, tiles_of(c - 1))


_INS = ['x', 'src', 'edge_attr_128', 'L0_gnn_W1', 'L0_gnn_b1', 'L0_gnn_W2', 'L0_gnn_b2']


def kernel(**inputs):
    import numpy as _np
    import concourse.bacc as _bacc
    from concourse import mybir as _mybir
    from concourse.bass_utils import run_bass_kernel_spmd as _run

    nc = _bacc.Bacc("TRN2", target_bir_lowering=False, num_devices=1)
    arrays, args = {}, []
    for name in _INS:
        a = _np.ascontiguousarray(inputs[name])
        arrays[f"in_{name}_dram"] = a
        args.append(nc.dram_tensor(f"in_{name}_dram", a.shape, _mybir.dt.from_np(a.dtype), kind="ExternalInput").ap())
    args.append(nc.dram_tensor("out_0_dram", inputs["x"].shape, _mybir.dt.float32, kind="ExternalOutput").ap())
    bass_segment_sum_resnorm_kernel(nc, *args)
    r = _run(nc, [arrays], core_ids=[0])
    return r.results[0]["out_0_dram"]
```
